# Optimizing a Trainium2 kernel written in Bass

```python
import numpy as np
import jax
import jax.numpy as jnp

def _softmax(x, axis=-1):
    return jax.nn.softmax(x, axis=axis)

def _gelu(x):
    return jax.nn.gelu(x, approximate=True)

def _silu(x):
    return jax.nn.silu(x)

def _sigmoid(x):
    return jax.nn.sigmoid(x)

def _layernorm(x, axis=-1, eps=1e-05):
    m = jnp.mean(x, axis=axis, keepdims=True)
    v = jnp.var(x, axis=axis, keepdims=True)
    return (x - m) / jnp.sqrt(v + eps)

def _scatter_add(tgt, idx, src, axis=0):
    return tgt.at[idx].add(src)

def _segment_sum(src, seg, n):
    return jax.ops.segment_sum(src, seg, n)
kernel_name = 'mk_dlrm_tower_d1_rec_r8_fd3d3f'

def setup_inputs(seed: int=0):
    np.random.seed(seed)
    _w = jnp.asarray

    def _rec_inputs():
        import jax
        import jax.numpy as jnp
        _tk = jax.random.key(seed)
        dense_ctx = jax.random.normal(jax.random.fold_in(_tk, 190), (2048, 16), jnp.float32)
        ids = jnp.stack([jax.random.randint(jax.random.fold_in(_tk, 200 + f), (2048,), 0, v, jnp.int32) for f, v in enumerate([1000, 1000, 1250, 12500, 1250, 125000, 125000, 12500, 12500, 1250, 1000, 1250, 1250, 1250, 12500, 125000, 1250, 1250, 1250, 1000, 1000, 12500, 12500, 1000, 12500, 1000, 1250, 1250, 1250, 1250, 1250, 1250])], axis=1)
        tbl_0 = 0.05 * jax.random.normal(jax.random.fold_in(_tk, 500 + 0), (1000, 64), jnp.float32)
        tbl_1 = 0.05 * jax.random.normal(jax.random.fold_in(_tk, 500 + 1), (1000, 64), jnp.float32)
        tbl_2 = 0.05 * jax.random.normal(jax.random.fold_in(_tk, 500 + 2), (1250, 64), jnp.float32)
        tbl_3 = 0.05 * jax.random.normal(jax.random.fold_in(_tk, 500 + 3), (12500, 64), jnp.float32)
        tbl_4 = 0.05 * jax.random.normal(jax.random.fold_in(_tk, 500 + 4), (1250, 64), jnp.float32)
        tbl_5 = 0.05 * jax.random.normal(jax.random.fold_in(_tk, 500 + 5), (125000, 64), jnp.float32)
        tbl_6 = 0.05 * jax.random.normal(jax.random.fold_in(_tk, 500 + 6), (125000, 64), jnp.float32)
        tbl_7 = 0.05 * jax.random.normal(jax.random.fold_in(_tk, 500 + 7), (12500, 64), jnp.float32)
        tbl_8 = 0.05 * jax.random.normal(jax.random.fold_in(_tk, 500 + 8), (12500, 64), jnp.float32)
        tbl_9 = 0.05 * jax.random.normal(jax.random.fold_in(_tk, 500 + 9), (1250, 64), jnp.float32)
        tbl_10 = 0.05 * jax.random.normal(jax.random.fold_in(_tk, 500 + 10), (1000, 64), jnp.float32)
        tbl_11 = 0.05 * jax.random.normal(jax.random.fold_in(_tk, 500 + 11), (1250, 64), jnp.float32)
        tbl_12 = 0.05 * jax.random.normal(jax.random.fold_in(_tk, 500 + 12), (1250, 64), jnp.float32)
        tbl_13 = 0.05 * jax.random.normal(jax.random.fold_in(_tk, 500 + 13), (1250, 64), jnp.float32)
        tbl_14 = 0.05 * jax.random.normal(jax.random.fold_in(_tk, 500 + 14), (12500, 64), jnp.float32)
        tbl_15 = 0.05 * jax.random.normal(jax.random.fold_in(_tk, 500 + 15), (125000, 64), jnp.float32)
        tbl_16 = 0.05 * jax.random.normal(jax.random.fold_in(_tk, 500 + 16), (1250, 64), jnp.float32)
        tbl_17 = 0.05 * jax.random.normal(jax.random.fold_in(_tk, 500 + 17), (1250, 64), jnp.float32)
        tbl_18 = 0.05 * jax.random.normal(jax.random.fold_in(_tk, 500 + 18), (1250, 64), jnp.float32)
        tbl_19 = 0.05 * jax.random.normal(jax.random.fold_in(_tk, 500 + 19), (1000, 64), jnp.float32)
        tbl_20 = 0.05 * jax.random.normal(jax.random.fold_in(_tk, 500 + 20), (1000, 64), jnp.float32)
        tbl_21 = 0.05 * jax.random.normal(jax.random.fold_in(_tk, 500 + 21), (12500, 64), jnp.float32)
        tbl_22 = 0.05 * jax.random.normal(jax.random.fold_in(_tk, 500 + 22), (12500, 64), jnp.float32)
        tbl_23 = 0.05 * jax.random.normal(jax.random.fold_in(_tk, 500 + 23), (1000, 64), jnp.float32)
        tbl_24 = 0.05 * jax.random.normal(jax.random.fold_in(_tk, 500 + 24), (12500, 64), jnp.float32)
        tbl_25 = 0.05 * jax.random.normal(jax.random.fold_in(_tk, 500 + 25), (1000, 64), jnp.float32)
        tbl_26 = 0.05 * jax.random.normal(jax.random.fold_in(_tk, 500 + 26), (1250, 64), jnp.float32)
        tbl_27 = 0.05 * jax.random.normal(jax.random.fold_in(_tk, 500 + 27), (1250, 64), jnp.float32)
        tbl_28 = 0.05 * jax.random.normal(jax.random.fold_in(_tk, 500 + 28), (1250, 64), jnp.float32)
        tbl_29 = 0.05 * jax.random.normal(jax.random.fold_in(_tk, 500 + 29), (1250, 64), jnp.float32)
        tbl_30 = 0.05 * jax.random.normal(jax.random.fold_in(_tk, 500 + 30), (1250, 64), jnp.float32)
        tbl_31 = 0.05 * jax.random.normal(jax.random.fold_in(_tk, 500 + 31), (1250, 64), jnp.float32)
        _rk = jax.random.fold_in(_tk, 7)
        W_top1 = 0.0441942 * jax.random.normal(jax.random.fold_in(_tk, 801), (512, 512), jnp.float32)
        W_top2 = 0.0441942 * jax.random.normal(jax.random.fold_in(_tk, 802), (512, 256), jnp.float32)
        W_top3 = 0.0625 * jax.random.normal(jax.random.fold_in(_tk, 803), (256, 1), jnp.float32)
        b_top1 = jnp.zeros((512,), jnp.float32)
        b_top2 = jnp.zeros((256,), jnp.float32)
        return (dense_ctx, ids, tbl_0, tbl_1, tbl_2, tbl_3, tbl_4, tbl_5, tbl_6, tbl_7, tbl_8, tbl_9, tbl_10, tbl_11, tbl_12, tbl_13, tbl_14, tbl_15, tbl_16, tbl_17, tbl_18, tbl_19, tbl_20, tbl_21, tbl_22, tbl_23, tbl_24, tbl_25, tbl_26, tbl_27, tbl_28, tbl_29, tbl_30, tbl_31, W_top1, b_top1, W_top2, b_top2, W_top3)
    dense_ctx, ids, tbl_0, tbl_1, tbl_2, tbl_3, tbl_4, tbl_5, tbl_6, tbl_7, tbl_8, tbl_9, tbl_10, tbl_11, tbl_12, tbl_13, tbl_14, tbl_15, tbl_16, tbl_17, tbl_18, tbl_19, tbl_20, tbl_21, tbl_22, tbl_23, tbl_24, tbl_25, tbl_26, tbl_27, tbl_28, tbl_29, tbl_30, tbl_31, W_top1, b_top1, W_top2, b_top2, W_top3 = _rec_inputs()

    def _L0_rec_setup():
        import jax, jax.numpy as jnp
        import numpy as np
        B, F, E = (512, 32, 64)
        P = F * (F - 1) // 2
        key = jax.random.key(seed)
        k1, k2 = jax.random.split(key)
        x = jax.random.normal(k1, (B, F, E), dtype=jnp.float32)
        kernel = jax.random.normal(k2, (E, P, E), dtype=jnp.float32) * 0.05
        return {'x': x, 'kernel': kernel}
    _L0_rec_all = _L0_rec_setup()
    _L0_rec_in = {k: v for k, v in _L0_rec_all.items() if k in ('kernel',)}
    del _L0_rec_all
    return {'dense_ctx': dense_ctx, 'ids': ids, 'tbl_0': tbl_0, 'tbl_1': tbl_1, 'tbl_2': tbl_2, 'tbl_3': tbl_3, 'tbl_4': tbl_4, 'tbl_5': tbl_5, 'tbl_6': tbl_6, 'tbl_7': tbl_7, 'tbl_8': tbl_8, 'tbl_9': tbl_9, 'tbl_10': tbl_10, 'tbl_11': tbl_11, 'tbl_12': tbl_12, 'tbl_13': tbl_13, 'tbl_14': tbl_14, 'tbl_15': tbl_15, 'tbl_16': tbl_16, 'tbl_17': tbl_17, 'tbl_18': tbl_18, 'tbl_19': tbl_19, 'tbl_20': tbl_20, 'tbl_21': tbl_21, 'tbl_22': tbl_22, 'tbl_23': tbl_23, 'tbl_24': tbl_24, 'tbl_25': tbl_25, 'tbl_26': tbl_26, 'tbl_27': tbl_27, 'tbl_28': tbl_28, 'tbl_29': tbl_29, 'tbl_30': tbl_30, 'tbl_31': tbl_31, 'W_top1': W_top1, 'b_top1': b_top1, 'W_top2': W_top2, 'b_top2': b_top2, 'W_top3': W_top3, 'L0_rec_kernel': _L0_rec_in['kernel']}

def reference(dense_ctx, ids, tbl_0, tbl_1, tbl_2, tbl_3, tbl_4, tbl_5, tbl_6, tbl_7, tbl_8, tbl_9, tbl_10, tbl_11, tbl_12, tbl_13, tbl_14, tbl_15, tbl_16, tbl_17, tbl_18, tbl_19, tbl_20, tbl_21, tbl_22, tbl_23, tbl_24, tbl_25, tbl_26, tbl_27, tbl_28, tbl_29, tbl_30, tbl_31, W_top1, b_top1, W_top2, b_top2, W_top3, L0_rec_kernel):
    import jax
    import jax.numpy as jnp

    def _L0_rec_ref(x, kernel):
        import jax, jax.numpy as jnp
        import numpy as np
        B, F, E = (512, 32, 64)
        P = F * (F - 1) // 2
        nf = x.shape[1]
        row_idx, col_idx = np.triu_indices(nf, k=1)
        p = x[:, row_idx, :]
        q = x[:, col_idx, :]
        kp = jnp.einsum('bpe,fpe,bpf->bp', p, kernel, q)
        return kp
    e = jnp.stack([tbl_0[ids[:, 0]], tbl_1[ids[:, 1]], tbl_2[ids[:, 2]], tbl_3[ids[:, 3]], tbl_4[ids[:, 4]], tbl_5[ids[:, 5]], tbl_6[ids[:, 6]], tbl_7[ids[:, 7]], tbl_8[ids[:, 8]], tbl_9[ids[:, 9]], tbl_10[ids[:, 10]], tbl_11[ids[:, 11]], tbl_12[ids[:, 12]], tbl_13[ids[:, 13]], tbl_14[ids[:, 14]], tbl_15[ids[:, 15]], tbl_16[ids[:, 16]], tbl_17[ids[:, 17]], tbl_18[ids[:, 18]], tbl_19[ids[:, 19]], tbl_20[ids[:, 20]], tbl_21[ids[:, 21]], tbl_22[ids[:, 22]], tbl_23[ids[:, 23]], tbl_24[ids[:, 24]], tbl_25[ids[:, 25]], tbl_26[ids[:, 26]], tbl_27[ids[:, 27]], tbl_28[ids[:, 28]], tbl_29[ids[:, 29]], tbl_30[ids[:, 30]], tbl_31[ids[:, 31]]], axis=1)
    z = _L0_rec_ref(e, L0_rec_kernel)
    z = z.reshape(z.shape[0], -1)
    h = jnp.concatenate([z, dense_ctx], axis=1)
    h = jnp.maximum(h @ W_top1 + b_top1, 0.0)
    h = jnp.maximum(h @ W_top2 + b_top2, 0.0)
    y = h @ W_top3
    return y

_drawn_inputs = setup_inputs


def setup_inputs(seed=0):
    import zlib

    import numpy as np

    out = dict(_drawn_inputs(seed))
    spreads = {'b_top1': (0.0, 0.1), 'b_top2': (0.0, 0.1)}
    factors = {'tbl_0': 6.411,
     'tbl_1': 6.147,
     'tbl_2': 5.83,
     'tbl_3': 5.56,
     'tbl_4': 4.783,
     'tbl_5': 6.163,
     'tbl_6': 5.811,
     'tbl_7': 4.851,
     'tbl_8': 5.701,
     'tbl_9': 5.501,
     'tbl_10': 5.629,
     'tbl_11': 5.298,
     'tbl_12': 5.386,
     'tbl_13': 5.036,
     'tbl_14': 5.854,
     'tbl_15': 5.466,
     'tbl_16': 5.235,
     'tbl_17': 5.766,
     'tbl_18': 5.137,
     'tbl_19': 5.536,
     'tbl_20': 5.433,
     'tbl_21': 5.701,
     'tbl_22': 5.942,
     'tbl_23': 5.769,
     'tbl_24': 5.762,
     'tbl_25': 5.344,
     'tbl_26': 5.616,
     'tbl_27': 5.485,
     'tbl_28': 6.007,
     'tbl_29': 5.548,
     'tbl_30': 5.655,
     'tbl_31': 6.104}
    for name, (base, spread) in spreads.items():
        noise = np.random.default_rng([zlib.crc32(name.encode()), seed]).standard_normal(out[name].shape)
        drawn = base * np.exp(spread * noise) if base else spread * noise
        out[name] = jnp.asarray(drawn.astype(out[name].dtype))
    for name, factor in factors.items():
        out[name] = (out[name] * factor).astype(out[name].dtype)
    return out
```

```python
from contextlib import ExitStack

import concourse.bass as bass
from concourse import mybir

F32 = mybir.dt.float32
F32R = mybir.dt.float32r
I32 = mybir.dt.int32
ALU = mybir.AluOpType
ACT = mybir.ActivationFunctionType

P = 128
BATCH, FIELDS, E = 2048, 32, 64
PAIRS = FIELDS * (FIELDS - 1) // 2
DENSE, H1, H2 = 16, 512, 256
CHUNK = 512
CHUNKS = BATCH // CHUNK
SUBS = CHUNK // P
GROUPS = FIELDS // 2

ROW_SLOTS = 4
SPLIT_SLOTS = 4
PROD_SLOTS = 3
STAGE_SLOTS = 3
STAGE_UNITS = 2
AHEAD = 4
DOUBLED_AHEAD = 2
KT = H1 // P
OT = H1 // P
HT = H2 // P
SEL_ROWS = 32
LAST_ROWS = SEL_ROWS - DENSE // 4


def plan_units():
    units = []
    for g in range(1, GROUPS):
        if g % 2:
            units.append(("diag", g // 2))
        units += [("full", a, g) for a in range(g)]
    return units


UNITS = plan_units()
NU = len(UNITS)
STAGES = NU // STAGE_UNITS
UNIT_AT = {u: n for n, u in enumerate(UNITS)}


def sum_plan():
    return [(n, x) for n, u in enumerate(UNITS) for x in range(1 if u[0] == "diag" else 2)]


SUMS = sum_plan()
PER_TILE = 4 * SEL_ROWS // 2


def pairs_of(n, x):
    u = UNITS[n]
    if u[0] == "diag":
        return [(4 * u[1], 4 * u[1] + 1), (4 * u[1] + 2, 4 * u[1] + 3)]
    return [(2 * u[1], 2 * u[2] + x), (2 * u[1] + 1, 2 * u[2] + x)]


def last_unit_of(f):
    if f == 0:
        return None
    return UNIT_AT[("diag", f // 4)] if f % 4 == 1 else UNIT_AT[("full", f // 2 - 1, f // 2)]


def plan_events():
    events = []
    for g in range(1, GROUPS):
        mine = [("unit", n) for n, u in enumerate(UNITS) if (u[0] == "diag" and 2 * u[1] + 1 == g) or
                (u[0] == "full" and u[2] == g)]
        mine.insert(1 if g < GROUPS - 1 else 3, ("prep", 2 * g + 2))
        mine.insert(3 if g < GROUPS - 1 else 6, ("prep", 2 * g + 3))
        events += mine
    return events + [("prep", FIELDS + f) for f in range(2, AHEAD)]


EVENTS = plan_events()


def plan_sums_at():
    at, issued = [], 0
    for kind, n in EVENTS:
        ready = sum(s[0] <= n - 2 for s in SUMS) if kind == "unit" else 0
        todo = []
        while ready - issued >= 4:
            todo += range(issued, issued + 4)
            issued += 4
        if kind == "unit" and issued < sum(s[0] <= n - PROD_SLOTS for s in SUMS):
            todo += range(issued, ready)
            issued = ready
        at.append(todo)
    return at, list(range(issued, len(SUMS)))


SUMS_AT, SUMS_LEFT = plan_sums_at()


def stage_target(n):
    return min(STAGES, 6 + 2 * n)


FIRST_STAGES = 6
STAGE_COLS = STAGE_UNITS * 2 * P
GROUP_OF = [2 * u[1] + 1 if u[0] == "diag" else u[2] for u in UNITS]
Z_LOADS = 5
MLP_LOADS = 2 + 4 + (CHUNKS - 1) * Z_LOADS


def tower_kernel(nc, ids, dense_t, k_units, w1, b1, w2, b2, w3, tables, y_out):
    ctx = ExitStack()
    with ctx:
        def sb(name, shape, dt=F32):
            return ctx.enter_context(nc.sbuf_tensor(name, shape, dt))

        def ps(name, shape):
            return ctx.enter_context(nc.psum_tensor(name, shape, F32))

        def sem(name):
            return ctx.enter_context(nc.semaphore(name))

        kw_at = -(-nc.sbuf_base // 32) * 32
        kw = sb("kw", [P, NU * 2 * P], F32R)
        x_pair = sb("x_pair", [P, GROUPS - 1, CHUNK])
        x_diag = sb("x_diag", [P, CHUNK])
        x_high = sb("x_high", [P, SPLIT_SLOTS, CHUNK], F32R)
        x_low = sb("x_low", [P, SPLIT_SLOTS, CHUNK], F32R)
        prod = sb("prod", [P, PROD_SLOTS, 2, CHUNK])
        rows = sb("rows", [P, ROW_SLOTS, SUBS, 2, E])
        z_out = sb("z_out", [P, CHUNK])
        k_raw = sb("k_raw", [P, STAGE_SLOTS, STAGE_UNITS * 2 * P])
        idx = sb("idx", [P, 2, FIELDS // 2 * SUBS], I32)
        ident = sb("ident", [P, P])
        sel = sb("sel", [P, 2 * SEL_ROWS])
        b1_sb = sb("b1_sb", [P, OT])
        b2_sb = sb("b2_sb", [P, HT])
        w3_sb = sb("w3_sb", [P, HT])


        taken = [kw_at]

        def over_kw(name, shape):
            t = nc.alloc_sbuf_tensor_at(name, shape, F32, offset=taken[0])
            n = 4
            for d in shape[1:]:
                n *= d
            taken[0] += n
            return t

        z_in = over_kw("z_in", [P, CHUNKS, KT, CHUNK])
        w1_sb = over_kw("w1_sb", [P, KT, H1])
        w2_sb = over_kw("w2_sb", [P, OT, H2])
        units_under_loads = -(-(taken[0] - kw_at) // (2 * P * 4))
        h1_sb = over_kw("h1_sb", [P, OT, CHUNK])
        h2_sb = over_kw("h2_sb", [P, HT, CHUNK])
        y_sb = over_kw("y_sb", [1, BATCH])
        assert taken[0] - kw_at <= NU * 2 * P * 4

        z_dram = nc.dram_tensor("z_scratch", [CHUNKS, KT, P, CHUNK], F32, kind="Internal").ap()

        t_ps = [ps(f"t_ps{i}", [P, 2, CHUNK]) for i in range(2)]
        z_ps = [ps(f"z_ps{i}", [P, CHUNK]) for i in range(2)]
        xt_ps = [ps(f"xt_ps{i}", [P, CHUNK]) for i in range(2)]

        idx_landed = [sem(f"idx_landed{i}") for i in range(2)]
        rows_landed = [sem(f"rows_landed{i}") for i in range(ROW_SLOTS)]
        k_landed = [sem(f"k_landed{i}") for i in range(STAGE_SLOTS)]
        small_landed = sem("small_landed")
        zeros_set = sem("zeros_set")
        ident_set = sem("ident_set")
        sel_zeros_set = sem("sel_zeros_set")
        sel_set = sem("sel_set")
        field_turn = sem("field_turn")
        rows_doubled = sem("rows_doubled")
        xt_ready = sem("xt_ready")
        x_copied = sem("x_copied")
        x_ready = sem("x_ready")
        k_high = sem("k_high")
        k_ready = sem("k_ready")
        t_ready = sem("t_ready")
        prod_ready = sem("prod_ready")
        prod_used = sem("prod_used")
        z_copied = sem("z_copied")
        z_stored = sem("z_stored")
        mlp_landed = sem("mlp_landed")
        z_last_landed = sem("z_last_landed")
        h1_summed = sem("h1_summed")
        h1_ready = sem("h1_ready")
        h2_summed = sem("h2_summed")
        h2_ready = sem("h2_ready")
        y_summed = sem("y_summed")
        y_ready = sem("y_ready")
        y_stored = sem("y_stored")

        block = ctx.enter_context(nc.Block())

        @block.sync
        def _(sp):
            def load_idx(c, half):
                sp.dma_start(idx[:, half, :], ids[c, half]).then_inc(idx_landed[half], 16)

            for half in range(2):
                load_idx(0, half)
            for s in range(STAGES):
                slot = s % STAGE_SLOTS
                if s >= STAGE_SLOTS:
                    sp.wait_ge(k_ready, s - STAGE_SLOTS + 1)
                src = k_units[:, s * STAGE_UNITS * 2 * P:(s + 1) * STAGE_UNITS * 2 * P]
                for half in range(2):
                    sp.dma_start(k_raw[64 * half:64 * half + 64, slot, :], src).then_inc(k_landed[slot], 16)
                if s == 4:
                    sp.dma_start(b1_sb[:, :], b1).then_inc(small_landed, 16)
                    sp.dma_start(b2_sb[:, :], b2).then_inc(small_landed, 16)
                    sp.dma_start(w3_sb[:, :], w3).then_inc(small_landed, 16)

            def store_z(c, k):
                sp.wait_ge(z_copied, c * KT + k + 1)
                sp.dma_start(z_dram[c, k], z_out[:, :]).then_inc(z_stored, 16)

            def next_idx(c, half):
                sp.wait_ge(rows_doubled, c * FIELDS + (half + 1) * (FIELDS // 2))
                load_idx(c + 1, half)

            def load_z(c, landed):
                sp.dma_start(z_in[:, c, 0:KT - 1, :], z_dram[c, 0:KT - 1].rearrange("k p b -> p k b")
                             ).then_inc(landed, 16)
                for q in range(4):
                    own = slice(SEL_ROWS * q, SEL_ROWS * q + LAST_ROWS)
                    sp.dma_start(z_in[own, c, KT - 1, :], z_dram[c, KT - 1, own, :]).then_inc(landed, 16)

            with sp.Fori(0, CHUNKS - 1) as c:
                store_z(c, 0)
                next_idx(c, 0)
                store_z(c, 1)
                store_z(c, 2)
                next_idx(c, 1)
                store_z(c, 3)
            store_z(CHUNKS - 1, 0)
            next_idx(CHUNKS - 1, 0)
            store_z(CHUNKS - 1, 1)
            sp.wait_ge(t_ready, (CHUNKS - 1) * NU + units_under_loads)
            sp.wait_ge(z_stored, (CHUNKS - 1) * KT * 16)
            sp.dma_start(w1_sb[:, :, :], w1).then_inc(mlp_landed, 16)
            sp.dma_start(w2_sb[:, :, :], w2).then_inc(mlp_landed, 16)
            for q in range(4):
                sp.dma_start(z_in[SEL_ROWS * q + LAST_ROWS:SEL_ROWS * (q + 1), :, KT - 1, :],
                             dense_t[q * (DENSE // 4):(q + 1) * (DENSE // 4), :].rearrange("d (c b) -> d c b", c=CHUNKS)
                             ).then_inc(mlp_landed, 16)
            for c in range(CHUNKS - 1):
                load_z(c, mlp_landed)
            store_z(CHUNKS - 1, 2)
            store_z(CHUNKS - 1, 3)
            sp.wait_ge(z_stored, CHUNKS * KT * 16)
            load_z(CHUNKS - 1, z_last_landed)

            sp.wait_ge(y_ready, CHUNKS)
            sp.dma_start(y_out, y_sb[:, :]).then_inc(y_stored, 16)
            sp.wait_ge(y_stored, 16)

        @block.gpsimd
        def _(pool):
            nc.gpsimd.memset(ident[:, :], 0.0).then_inc(zeros_set, 1)
            pool.wait_ge(zeros_set, 1)
            nc.gpsimd.affine_select(out=ident[:, :], in_=ident[:, :], compare_op=ALU.not_equal, fill=1.0,
                                    base=0, pattern=[[-1, P]], channel_multiplier=1).then_inc(ident_set, 1)

            def gather(c, f, first):
                half, at = f // (FIELDS // 2), f % (FIELDS // 2)
                if at == 0:
                    pool.wait_ge(idx_landed[half], c * 16 + 16)
                if not first or f >= ROW_SLOTS:
                    pool.wait_ge(xt_ready, c * FIELDS + f - ROW_SLOTS + 1)
                pool.sem_inc(field_turn, 1)
                for t in range(SUBS):
                    nc.gpsimd.indirect_dma_start(
                        out=rows[:, f % ROW_SLOTS, t, 0, :], out_offset=None, in_=tables[f],
                        in_offset=bass.IndirectOffsetOnAxis(ap=idx[:, half, at * SUBS + t:at * SUBS + t + 1], axis=0),
                    ).then_inc(rows_landed[f % ROW_SLOTS], 16)

            for f in range(FIELDS):
                gather(0, f, True)
            with pool.Fori(1, CHUNKS) as c:
                for f in range(FIELDS):
                    gather(c, f, False)
            for f in range(AHEAD + DOUBLED_AHEAD):
                gather(CHUNKS, f, False)

        @block.scalar
        def _(act):
            def double_rows(c, f):
                gathers = (c * (FIELDS // ROW_SLOTS) + f // ROW_SLOTS + 1) * SUBS
                act.wait_ge(rows_landed[f % ROW_SLOTS], gathers * 16)
                nc.scalar.activation(rows[:, f % ROW_SLOTS, :, 1, :], rows[:, f % ROW_SLOTS, :, 0, :],
                                     ACT.Copy).then_inc(rows_doubled, 1)

            def split_high(s):
                act.wait_ge(k_landed[s % STAGE_SLOTS], 32 * (s // STAGE_SLOTS + 1))
                nc.scalar.activation(kw[:, s * STAGE_COLS:(s + 1) * STAGE_COLS], k_raw[:, s % STAGE_SLOTS, :],
                                     ACT.Copy).then_inc(k_high, 1)

            def copy_field(c, f):
                act.wait_ge(xt_ready, c * FIELDS + f + 1)
                xt, g = xt_ps[f % 2], f % FIELDS // 2
                if f >= SPLIT_SLOTS and f != SPLIT_SLOTS:
                    act.wait_ge(t_ready, c * NU + last_unit_of(f - SPLIT_SLOTS) + 1)
                if f % 2 == 0:
                    side = slice(64, 128) if f % 4 else slice(0, 64)
                    if f >= 4:
                        act.wait_ge(prod_ready, c * NU + UNIT_AT[("diag", f // 4 - 1)] + 1)
                    nc.scalar.activation(x_diag[side, :], xt[side, :], ACT.Copy)
                if g < GROUPS - 1:
                    side = slice(64, 128) if f % 2 else slice(0, 64)
                    if f >= FIELDS:
                        act.wait_ge(prod_ready, c * NU + UNIT_AT[("full", g, GROUPS - 1)] + 1)
                    nc.scalar.activation(x_pair[side, g, :], xt[side, :], ACT.Copy)
                nc.scalar.activation(x_high[:, f % SPLIT_SLOTS, :], xt[:, :], ACT.Copy).then_inc(x_copied, 1)

            def copy_z(c, k, first):
                last_sum = min((k + 1) * PER_TILE, len(SUMS)) - 1
                act.wait_ge(prod_used, c * NU + SUMS[last_sum][0] + 1)
                if not first or k >= 1:
                    act.wait_ge(z_stored, (c * KT + k) * 16)
                nc.scalar.activation(z_out[:, :], z_ps[k % 2][:, :], ACT.Copy).then_inc(z_copied, 1)

            def chunk(c, first):
                staged, issued, copied = FIRST_STAGES, 0, 0
                for todo, (kind, n) in zip(SUMS_AT, EVENTS):
                    if kind == "unit":
                        while first and staged < stage_target(n):
                            split_high(staged)
                            staged += 1
                    else:
                        copy_field(c, n)
                        double_rows(c, n + DOUBLED_AHEAD)
                    if copied < (issued - 1) // PER_TILE:
                        copy_z(c, copied, first)
                        copied += 1
                    issued += len(todo)
                for k in range(copied, KT):
                    copy_z(c, k, first)

            for f in range(DOUBLED_AHEAD):
                double_rows(0, f)
            for s in range(FIRST_STAGES):
                split_high(s)
            for f in range(AHEAD):
                copy_field(0, f)
                double_rows(0, f + DOUBLED_AHEAD)
            chunk(0, True)
            with act.Fori(1, CHUNKS) as c:
                chunk(c, False)

            def relu_1(n, first):
                for o in range(OT):
                    act.wait_ge(h1_summed, n * OT + o + 1)
                    if not first and o == 0:
                        act.wait_ge(h2_summed, n * HT)
                    nc.scalar.activation(h1_sb[:, o, :], t_ps[o // 2][:, o % 2, :], ACT.Relu,
                                         bias=b1_sb[:, o:o + 1]).then_inc(h1_ready, 1)

            def relu_2(n, first):
                for o in range(HT):
                    act.wait_ge(h2_summed, n * HT + o + 1)
                    if not first and o == 0:
                        act.wait_ge(y_summed, n)
                    nc.scalar.activation(h2_sb[:, o, :], z_ps[o][:, :], ACT.Relu,
                                         bias=b2_sb[:, o:o + 1]).then_inc(h2_ready, 1)

            act.wait_ge(small_landed, 48)
            relu_1(0, True)
            relu_2(0, True)
            with act.Fori(1, CHUNKS - 1) as n:
                relu_1(n, False)
                relu_2(n, False)
            relu_1(CHUNKS - 1, False)
            relu_2(CHUNKS - 1, False)

        @block.vector
        def _(dve):
            def split_low(s):
                cols = slice(s * STAGE_COLS, (s + 1) * STAGE_COLS)
                dve.wait_ge(k_high, s + 1)
                nc.vector.tensor_tensor(kw[64:128, cols], k_raw[64:128, s % STAGE_SLOTS, :],
                                        kw[64:128, cols].bitcast(F32), ALU.subtract).then_inc(k_ready, 1)

            def low_part(c, f):
                dve.wait_ge(x_copied, c * FIELDS + f + 1)
                slot = f % SPLIT_SLOTS
                nc.vector.tensor_tensor(x_low[:, slot, :], xt_ps[f % 2][:, :], x_high[:, slot, :].bitcast(F32),
                                        ALU.subtract).then_inc(x_ready, 1)

            def multiply(c, n, first):
                dve.wait_ge(t_ready, c * NU + n + 1)
                if n >= PROD_SLOTS:
                    dve.wait_ge(prod_used, c * NU + n - PROD_SLOTS + 1)
                elif not first:
                    dve.wait_ge(prod_used, c * NU)
                if UNITS[n][0] == "diag":
                    nc.vector.tensor_tensor(prod[:, n % PROD_SLOTS, 0, :], t_ps[n % 2][:, 0, :], x_diag[:, :],
                                            ALU.mult).then_inc(prod_ready, 1)
                else:
                    x_i = x_pair[:, UNITS[n][1]:UNITS[n][1] + 1, :].to_broadcast([P, 2, CHUNK])
                    nc.vector.tensor_tensor(prod[:, n % PROD_SLOTS, :, :], t_ps[n % 2][:, :, :], x_i,
                                            ALU.mult).then_inc(prod_ready, 1)

            def chunk(c, first):
                staged = FIRST_STAGES
                for kind, n in EVENTS:
                    if kind == "unit":
                        while first and staged < stage_target(n):
                            split_low(staged)
                            staged += 1
                        multiply(c, n, first)
                    else:
                        low_part(c, n)

            nc.vector.memset(sel[:, :], 0.0).then_inc(sel_zeros_set, 1)
            dve.wait_ge(sel_zeros_set, 1)
            nc.vector.memset(sel[0:64, SEL_ROWS - 2:SEL_ROWS - 1], 1.0).then_inc(sel_set, 1)
            nc.vector.memset(sel[64:128, SEL_ROWS - 1:SEL_ROWS], 1.0).then_inc(sel_set, 1)
            for s in range(FIRST_STAGES):
                split_low(s)
            for f in range(AHEAD):
                low_part(0, f)
            chunk(0, True)
            with dve.Fori(1, CHUNKS) as c:
                chunk(c, False)
            with dve.Fori(0, CHUNKS) as n:
                dve.wait_ge(y_summed, n + 1)
                nc.vector.tensor_copy(y_sb[0:1, bass.ds(n * CHUNK, CHUNK)], xt_ps[0][0:1, :]).then_inc(y_ready, 1)

        @block.tensor
        def _(pe):
            def transpose(c, f, first):
                pe.wait_ge(rows_doubled, c * FIELDS + f + 1)
                if not first or f >= 2:
                    pe.wait_ge(x_ready, c * FIELDS + f - 1)
                for t in range(SUBS):
                    last = nc.tensor.transpose(xt_ps[f % 2][:, t * P:(t + 1) * P],
                                               rows[:, f % ROW_SLOTS, t, :, :].rearrange("p a e -> p (a e)"),
                                               ident[:, :])
                last.then_inc(xt_ready, 1)

            def contract(c, n, first):
                u = UNITS[n]
                if not first or n >= 2:
                    pe.wait_ge(prod_ready, c * NU + n - 1)
                if n == 0 or GROUP_OF[n] != GROUP_OF[n - 1]:
                    pe.wait_ge(x_ready, c * FIELDS + 2 * GROUP_OF[n] + 2)
                if first and n % STAGE_UNITS == 0:
                    pe.wait_ge(k_ready, n // STAGE_UNITS + 1)
                for x in range(2):
                    k_part = kw[:, (2 * n + x) * P:(2 * n + x + 1) * P]
                    diag = u[0] == "diag"
                    out = t_ps[n % 2][:, 0 if diag else x, :]
                    slot = (4 * u[1] + 1 + 2 * x if diag else 2 * u[2] + x) % SPLIT_SLOTS
                    nc.tensor.matmul(out, k_part, x_high[:, slot, :], start=not (diag and x), stop=False)
                    last = nc.tensor.matmul(out, k_part, x_low[:, slot, :], start=False, stop=not (diag and not x))
                last.then_inc(t_ready, 1)

            def sum_over_e(c, m, first):
                n, x = SUMS[m]
                k, q, r = m // PER_TILE, m % 4, m % PER_TILE // 4
                if m % PER_TILE == 0 and not (first and k < 2):
                    pe.wait_ge(z_copied, c * KT + k - 1)
                if x == 0:
                    pe.wait_ge(prod_ready, c * NU + n + 1)
                mm = nc.tensor.matmul(z_ps[k % 2][SEL_ROWS * q:SEL_ROWS * (q + 1), :],
                                      sel[:, SEL_ROWS - 2 - 2 * r:2 * SEL_ROWS - 2 - 2 * r], prod[:, n % PROD_SLOTS, x, :],
                                      start=r == 0, stop=m + 4 >= len(SUMS) or r == PER_TILE // 4 - 1)
                if m == len(SUMS) - 1 or SUMS[m + 1][0] != n:
                    mm.then_inc(prod_used, 1)

            def chunk(c, first):
                for todo, (kind, n) in zip(SUMS_AT, EVENTS):
                    if kind == "unit":
                        contract(c, n, first)
                    else:
                        transpose(c, n, first)
                    for m in todo:
                        sum_over_e(c, m, first)
                for m in SUMS_LEFT:
                    sum_over_e(c, m, first)

            pe.wait_ge(ident_set, 1)
            pe.wait_ge(sel_set, 2)
            for f in range(AHEAD):
                transpose(0, f, True)
            chunk(0, True)
            with pe.Fori(1, CHUNKS) as c:
                chunk(c, False)

            def layer_1(n, first):
                for o in range(OT):
                    if not first:
                        pe.wait_ge(h1_ready, (n - 1) * OT + o + 1)
                    for k in range(KT):
                        last = nc.tensor.matmul(t_ps[o // 2][:, o % 2, :], w1_sb[:, k, o * P:(o + 1) * P],
                                                z_in[:, n, k, :], start=k == 0, stop=k == KT - 1)
                    last.then_inc(h1_summed, 1)

            def layer_2(n, first):
                pe.wait_ge(h1_ready, (n + 1) * OT)
                for o in range(HT):
                    if not first:
                        pe.wait_ge(h2_ready, (n - 1) * HT + o + 1)
                    for k in range(OT):
                        last = nc.tensor.matmul(z_ps[o][:, :], w2_sb[:, k, o * P:(o + 1) * P], h1_sb[:, k, :],
                                                start=k == 0, stop=k == OT - 1)
                    last.then_inc(h2_summed, 1)

            def layer_3(n, first):
                pe.wait_ge(h2_ready, (n + 1) * HT)
                if not first:
                    pe.wait_ge(y_ready, n)
                for k in range(HT):
                    last = nc.tensor.matmul(xt_ps[0][0:1, :], w3_sb[:, k:k + 1], h2_sb[:, k, :],
                                            start=k == 0, stop=k == HT - 1)
                last.then_inc(y_summed, 1)

            pe.wait_ge(mlp_landed, 16 * MLP_LOADS)
            pe.wait_ge(z_copied, CHUNKS * KT)
            pe.wait_ge(x_ready, CHUNKS * FIELDS + AHEAD)
            pe.wait_ge(small_landed, 48)
            layer_1(0, True)
            layer_1(1, False)
            layer_2(0, True)
            layer_3(0, True)
            with pe.Fori(2, CHUNKS - 1) as n:
                layer_1(n, False)
                layer_2(n - 1, False)
                layer_3(n - 1, False)
            pe.wait_ge(z_last_landed, 16 * Z_LOADS)
            layer_1(CHUNKS - 1, False)
            for n in range(CHUNKS - 2, CHUNKS):
                layer_2(n, False)
                layer_3(n, False)


def kernel(**inputs):
    import numpy as np
    import concourse.bacc as bacc
    from concourse.bass_utils import run_bass_kernel_spmd

    ids = np.asarray(inputs["ids"])
    by_chunk = ids.reshape(CHUNKS, SUBS, P, 2, FIELDS // 2).transpose(0, 3, 2, 4, 1)
    by_chunk = by_chunk.reshape(CHUNKS, 2, P, FIELDS // 2 * SUBS)
    by_chunk = np.concatenate([by_chunk, by_chunk[:1]], axis=0)

    pair_at = {}
    for n, (i, j) in enumerate(zip(*np.triu_indices(FIELDS, k=1))):
        pair_at[int(i), int(j)] = n

    k = np.asarray(inputs["L0_rec_kernel"])
    k_units = np.zeros((E, NU, 2, 2, E), k.dtype)
    for n, u in enumerate(UNITS):
        if u[0] == "diag":
            for x, pair in enumerate(pairs_of(n, 0)):
                k_units[:, n, x, x] = k[:, pair_at[pair]]
        else:
            for x in range(2):
                for y, pair in enumerate(pairs_of(n, x)):
                    k_units[:, n, x, y] = k[:, pair_at[pair]]

    w1 = np.asarray(inputs["W_top1"])
    order = np.zeros((KT, 4, SEL_ROWS), np.int64)
    for m, (n, x) in enumerate(SUMS):
        for y, pair in enumerate(pairs_of(n, x)):
            order[m // PER_TILE, m % 4, 2 * (m % PER_TILE // 4) + y] = pair_at[pair]
    order[KT - 1, :, LAST_ROWS:] = PAIRS + np.arange(DENSE).reshape(4, DENSE // 4)

    def tiles(a, n):
        return np.ascontiguousarray(a.reshape(n, P, -1).transpose(1, 0, 2))

    arrays = {
        "ids": by_chunk,
        "dense_t": np.asarray(inputs["dense_ctx"]).T,
        "k_units": k_units.reshape(E, NU * 2 * P),
        "w1": tiles(w1[order.reshape(-1)], KT),
        "b1": np.asarray(inputs["b_top1"]).reshape(OT, P).T,
        "w2": tiles(np.asarray(inputs["W_top2"]), OT),
        "b2": np.asarray(inputs["b_top2"]).reshape(HT, P).T,
        "w3": np.asarray(inputs["W_top3"]).reshape(HT, P).T,
    }
    arrays |= {f"tbl_{f}": np.asarray(inputs[f"tbl_{f}"]) for f in range(FIELDS)}
    arrays = {name: np.ascontiguousarray(a) for name, a in arrays.items()}

    nc = bacc.Bacc("TRN2", target_bir_lowering=False, num_devices=1)
    ap = {name: nc.dram_tensor(f"{name}_dram", a.shape, mybir.dt.from_np(a.dtype), kind="ExternalInput").ap()
          for name, a in arrays.items()}
    y = nc.dram_tensor("y_dram", (1, BATCH), F32, kind="ExternalOutput").ap()
    tower_kernel(nc, ap["ids"], ap["dense_t"], ap["k_units"], ap["w1"], ap["b1"], ap["w2"], ap["b2"], ap["w3"],
                 [ap[f"tbl_{f}"] for f in range(FIELDS)], y)
    r = run_bass_kernel_spmd(nc, [{f"{name}_dram": a for name, a in arrays.items()}], core_ids=[0])
    return r.results[0]["y_dram"].reshape(BATCH, 1)
```

```python
from contextlib import ExitStack

import concourse.bass as bass
from concourse import mybir

F32 = mybir.dt.float32
F32R = mybir.dt.float32r
I32 = mybir.dt.int32
ALU = mybir.AluOpType
ACT = mybir.ActivationFunctionType

P = 128
BATCH, FIELDS, E = 2048, 32, 64
PAIRS = FIELDS * (FIELDS - 1) // 2
DENSE, H1, H2 = 16, 512, 256
CHUNK = 512
CHUNKS = BATCH // CHUNK
SUBS = CHUNK // P
GROUPS = FIELDS // 2

ROW_SLOTS = 8
TWICE_SLOTS = 2
SPLIT_SLOTS = 5
PROD_SLOTS = 4
RAW_UNDER = 8
STAGE_SLOTS = GROUPS - 1 - RAW_UNDER
AHEAD = 6
DOUBLED_AHEAD = 2
EARLY_FIELDS = 10
NEXT_AT = [3, 5, 8, 10, 12, 14]
FIRST_AT = {6: 0, 7: 1, 8: 3, 9: 4, 10: 6, 11: 8}
DELAY = 2
FIRST_STAGES = [8, 10, 14, 18, 22, 24, 26]
KT = H1 // P
OT = H1 // P
HT = H2 // P
SEL_ROWS = 32
LAST_ROWS = SEL_ROWS - DENSE // 4


def plan_units():
    units = []
    for g in range(1, GROUPS):
        if g % 2:
            units.append(("diag", g // 2))
        units += [("full", a, g) for a in range(g)]
    return units


UNITS = plan_units()
NU = len(UNITS)
UNIT_COLS = [3 * E if u[0] == "diag" else 4 * E for u in UNITS]
COL_OF = [sum(UNIT_COLS[:n]) for n in range(NU)]
KW_COLS = sum(UNIT_COLS)
STAGE_RATE = [0, 3, 3, 2, 1.3, .8, .4, .4]
STAGE_COLS = 8 * E
STAGES = -(-KW_COLS // STAGE_COLS)
UNIT_AT = {u: n for n, u in enumerate(UNITS)}
GROUP_OF = [2 * u[1] + 1 if u[0] == "diag" else u[2] for u in UNITS]


def sum_plan():
    return [(n, x) for n, u in enumerate(UNITS) for x in range(1 if u[0] == "diag" else 2)]


SUMS = sum_plan()
PER_TILE = 4 * SEL_ROWS // 2


def pairs_of(n, x):
    u = UNITS[n]
    if u[0] == "diag":
        return [(4 * u[1], 4 * u[1] + 1), (4 * u[1] + 2, 4 * u[1] + 3)]
    return [(2 * u[1], 2 * u[2] + x), (2 * u[1] + 1, 2 * u[2] + x)]


def plan_slots():
    slots = [None, 1, 2, 4]
    for g in range(2, GROUPS):
        slots += {3: (1, 2), 4: (4, 0), 5: (3, 1), 6: (2, 4)}.get(g, (1, 2) if g % 2 == 0 and g > 2 else (0, 3))
    return slots


SLOT_OF = plan_slots()


def last_unit_of(f):
    return UNIT_AT[("diag", f // 4)] if f % 4 == 1 else UNIT_AT[("full", f // 2 - 1, f // 2)]


def slot_free_after(f):
    for before in range(f - 1, max(0, f - FIELDS), -1):
        if SLOT_OF[before % FIELDS] == SLOT_OF[f % FIELDS]:
            return last_unit_of(before) if before < FIELDS else None
    return None


def plan_events():
    after, at = {}, 0
    for f in range(AHEAD, FIELDS + AHEAD):
        g = f // 2 - 1
        if f in FIRST_AT:
            at = FIRST_AT[f]
        elif f < FIELDS:
            start = GROUP_OF.index(g)
            at = start + ((1 if f % 2 == 0 else g // 2) if g > 6 else (0 if f % 2 == 0 else 2))
        else:
            at = UNIT_AT[("full", 0, GROUPS - 1)] + NEXT_AT[f - FIELDS]
        if slot_free_after(f) is not None: assert at >= slot_free_after(f) or f>=FIELDS, f
        after.setdefault(at, []).append(f)
    events = []
    for n in range(NU):
        events += [("unit", n)] + [("prep", f) for f in after.get(n, [])]
    return events


EVENTS = plan_events()


def plan_vector_events():
    at, unit = {}, 0
    for kind, n in EVENTS:
        if kind == "unit":
            unit = n
        else:
            at[n] = unit
    events = [e for e in EVENTS if e[0] == "unit"]
    for f in reversed(at):
        group_starts = GROUP_OF.index(f // 2) if f < FIELDS else NU
        late = max(at[f], min(at[f] + DELAY, group_starts - 2, at.get(f + 2, NU)))
        events.insert(events.index(("unit", late)) + 1, ("prep", f))
    return events


VECTOR_EVENTS = plan_vector_events()


def plan_sums_at():
    at, issued = [], 0
    for kind, n in EVENTS:
        ready = sum(s[0] <= n - 2 for s in SUMS) if kind == "unit" else 0
        todo = []
        while ready - issued >= 4:
            todo += range(issued, issued + 4)
            issued += 4
        if kind == "unit" and issued < sum(s[0] <= n - PROD_SLOTS + 1 for s in SUMS):
            todo += range(issued, ready)
            issued = ready
        at.append(todo)
    return at, list(range(issued, len(SUMS)))


SUMS_AT, SUMS_LEFT = plan_sums_at()


def stages_of(n):
    return -(-(COL_OF[n] + UNIT_COLS[n]) // STAGE_COLS)


def stage_target(n):
    last = [e for e in EVENTS[:EVENTS.index(("prep", 2 * RAW_UNDER))] if e[0] == "unit"][-1][1]
    at = [FIRST_STAGES[-1]]
    for m in range(last + 1):
        at.append(at[-1] + STAGE_RATE[min(GROUP_OF[m],len(STAGE_RATE)-1)])
    return min(STAGES, int(at[n + 1] if n < last else STAGES))


Z_LOADS = 5
MLP_LOADS = 2 + 4 + (CHUNKS - 1) * Z_LOADS


def tower_kernel(nc, ids, dense_t, k_units, w1, b1, w2, b2, w3, tables, y_out):
    ctx = ExitStack()
    with ctx:
        def sb(name, shape, dt=F32):
            return ctx.enter_context(nc.sbuf_tensor(name, shape, dt))

        def ps(name, shape):
            return ctx.enter_context(nc.psum_tensor(name, shape, F32))

        def sem(name):
            return ctx.enter_context(nc.semaphore(name))

        kw_at = -(-nc.sbuf_base // 32) * 32
        kw = sb("kw", [P, KW_COLS], F32R)
        x_pair_at = -(-nc.sbuf_base // 32) * 32
        x_pair = sb("x_pair", [P, GROUPS - 1, CHUNK])
        z_out = sb("z_out", [P, CHUNK])
        x_high = sb("x_high", [P, SPLIT_SLOTS, CHUNK], F32R)
        x_low = sb("x_low", [P, SPLIT_SLOTS, CHUNK], F32R)
        prod = sb("prod", [P, PROD_SLOTS, 2, CHUNK])
        rows = sb("rows", [P, ROW_SLOTS, SUBS, E])
        rows_twice = sb("rows_twice", [P, TWICE_SLOTS, SUBS, 2, E])
        idx = sb("idx", [P, 2, FIELDS // 2 * SUBS], I32)
        ident = sb("ident", [P, P])
        sel = sb("sel", [P, 2 * SEL_ROWS])
        b1_sb = sb("b1_sb", [P, OT])
        b2_sb = sb("b2_sb", [P, HT])
        w3_sb = sb("w3_sb", [P, HT])


        k_raw = nc.alloc_sbuf_tensor_at("k_raw", [P, STAGE_SLOTS, STAGE_COLS], F32,
                                        offset=x_pair_at + RAW_UNDER * CHUNK * 4)

        taken = [kw_at]

        def over_kw(name, shape):
            t = nc.alloc_sbuf_tensor_at(name, shape, F32, offset=taken[0])
            n = 4
            for d in shape[1:]:
                n *= d
            taken[0] += n
            return t

        z_in = over_kw("z_in", [P, CHUNKS, KT, CHUNK])
        w1_sb = over_kw("w1_sb", [P, KT, H1])
        w2_sb = over_kw("w2_sb", [P, OT, H2])
        units_under_loads = sum(4 * col < taken[0] - kw_at for col in COL_OF)
        h1_sb = over_kw("h1_sb", [P, OT, CHUNK])
        h2_sb = over_kw("h2_sb", [P, HT, CHUNK])
        y_sb = over_kw("y_sb", [1, BATCH])
        assert taken[0] - kw_at <= KW_COLS * 4

        z_dram = nc.dram_tensor("z_scratch", [CHUNKS, KT, P, CHUNK], F32, kind="Internal").ap()

        t_ps = [ps(f"t_ps{i}", [P, 2, CHUNK]) for i in range(2)]
        z_ps = [ps(f"z_ps{i}", [P, CHUNK]) for i in range(2)]
        xt_ps = [ps(f"xt_ps{i}", [P, CHUNK]) for i in range(2)]

        idx_landed = [sem(f"idx_landed{i}") for i in range(2)]
        rows_landed = [sem(f"rows_landed{i}") for i in range(ROW_SLOTS)]
        k_landed = [sem(f"k_landed{i}") for i in range(STAGE_SLOTS)]
        small_landed = sem("small_landed")
        zeros_set = sem("zeros_set")
        ident_set = sem("ident_set")
        sel_zeros_set = sem("sel_zeros_set")
        sel_set = sem("sel_set")
        field_turn = sem("field_turn")
        rows_doubled = sem("rows_doubled")
        xt_ready = sem("xt_ready")
        x_copied = sem("x_copied")
        x_ready = sem("x_ready")
        k_high = sem("k_high")
        k_ready = sem("k_ready")
        t_ready = sem("t_ready")
        prod_ready = sem("prod_ready")
        prod_used = sem("prod_used")
        z_copied = sem("z_copied")
        z_stored = sem("z_stored")
        mlp_landed = sem("mlp_landed")
        z_last_landed = sem("z_last_landed")
        h1_summed = sem("h1_summed")
        h1_ready = sem("h1_ready")
        h2_summed = sem("h2_summed")
        h2_ready = sem("h2_ready")
        y_summed = sem("y_summed")
        y_ready = sem("y_ready")
        y_stored = sem("y_stored")

        block = ctx.enter_context(nc.Block())

        @block.sync
        def _(sp):
            def load_idx(c, half):
                sp.dma_start(idx[:, half, :], ids[c, half]).then_inc(idx_landed[half], 16)

            for half in range(2):
                load_idx(0, half)
            for s in range(STAGES):
                slot = s % STAGE_SLOTS
                if s >= STAGE_SLOTS:
                    sp.wait_ge(k_ready, s - STAGE_SLOTS + 1)
                lo, hi = s * STAGE_COLS, min((s + 1) * STAGE_COLS, KW_COLS)
                for half in range(2):
                    sp.dma_start(k_raw[64 * half:64 * half + 64, slot, 0:hi - lo], k_units[:, lo:hi]).then_inc(k_landed[slot], 16)
                if s == 4:
                    sp.dma_start(b1_sb[:, :], b1).then_inc(small_landed, 16)
                    sp.dma_start(b2_sb[:, :], b2).then_inc(small_landed, 16)
                    sp.dma_start(w3_sb[:, :], w3).then_inc(small_landed, 16)

            def store_z(c, k):
                sp.wait_ge(z_copied, c * KT + k + 1)
                sp.dma_start(z_dram[c, k], z_out[:, :]).then_inc(z_stored, 16)

            def next_idx(c, half):
                sp.wait_ge(rows_doubled, c * FIELDS + (half + 1) * (FIELDS // 2))
                load_idx(c + 1, half)

            def load_z(c, landed):
                sp.dma_start(z_in[:, c, 0:KT - 1, :], z_dram[c, 0:KT - 1].rearrange("k p b -> p k b")
                             ).then_inc(landed, 16)
                for q in range(4):
                    own = slice(SEL_ROWS * q, SEL_ROWS * q + LAST_ROWS)
                    sp.dma_start(z_in[own, c, KT - 1, :], z_dram[c, KT - 1, own, :]).then_inc(landed, 16)

            with sp.Fori(0, CHUNKS - 1) as c:
                store_z(c, 0)
                next_idx(c, 0)
                store_z(c, 1)
                store_z(c, 2)
                next_idx(c, 1)
                store_z(c, 3)
            store_z(CHUNKS - 1, 0)
            next_idx(CHUNKS - 1, 0)
            store_z(CHUNKS - 1, 1)
            sp.wait_ge(t_ready, (CHUNKS - 1) * NU + units_under_loads)
            sp.wait_ge(z_stored, (CHUNKS - 1) * KT * 16)
            sp.dma_start(w1_sb[:, :, :], w1).then_inc(mlp_landed, 16)
            sp.dma_start(w2_sb[:, :, :], w2).then_inc(mlp_landed, 16)
            for q in range(4):
                sp.dma_start(z_in[SEL_ROWS * q + LAST_ROWS:SEL_ROWS * (q + 1), :, KT - 1, :],
                             dense_t[q * (DENSE // 4):(q + 1) * (DENSE // 4), :].rearrange("d (c b) -> d c b", c=CHUNKS)
                             ).then_inc(mlp_landed, 16)
            for c in range(CHUNKS - 1):
                load_z(c, mlp_landed)
            store_z(CHUNKS - 1, 2)
            store_z(CHUNKS - 1, 3)
            sp.wait_ge(z_stored, CHUNKS * KT * 16)
            load_z(CHUNKS - 1, z_last_landed)

            sp.wait_ge(y_ready, CHUNKS)
            sp.dma_start(y_out, y_sb[:, :]).then_inc(y_stored, 16)
            sp.wait_ge(y_stored, 16)

        @block.gpsimd
        def _(pool):
            nc.gpsimd.memset(ident[:, :], 0.0).then_inc(zeros_set, 1)
            pool.wait_ge(zeros_set, 1)
            nc.gpsimd.affine_select(out=ident[:, :], in_=ident[:, :], compare_op=ALU.not_equal, fill=1.0,
                                    base=0, pattern=[[-1, P]], channel_multiplier=1).then_inc(ident_set, 1)

            def gather(c, f, first):
                half, at = f // (FIELDS // 2), f % (FIELDS // 2)
                if at == 0:
                    pool.wait_ge(idx_landed[half], c * 16 + 16)
                if not first or f >= ROW_SLOTS:
                    pool.wait_ge(rows_doubled, c * FIELDS + f - ROW_SLOTS + 1)
                pool.sem_inc(field_turn, 1)
                for t in range(SUBS):
                    nc.gpsimd.indirect_dma_start(
                        out=rows[:, f % ROW_SLOTS, t, :], out_offset=None, in_=tables[f],
                        in_offset=bass.IndirectOffsetOnAxis(ap=idx[:, half, at * SUBS + t:at * SUBS + t + 1], axis=0),
                    ).then_inc(rows_landed[f % ROW_SLOTS], 16)

            for f in range(FIELDS):
                gather(0, f, True)
            with pool.Fori(1, CHUNKS) as c:
                for f in range(FIELDS):
                    gather(c, f, False)
            for f in range(AHEAD + DOUBLED_AHEAD):
                gather(CHUNKS, f, False)

        @block.scalar
        def _(act):
            def double_rows(c, f):
                gathers = (c * (FIELDS // ROW_SLOTS) + f // ROW_SLOTS + 1) * SUBS
                act.wait_ge(rows_landed[f % ROW_SLOTS], gathers * 16)
                nc.scalar.activation(rows_twice[:, f % TWICE_SLOTS, :, :, :],
                                     rows[:, f % ROW_SLOTS, :, None, :].to_broadcast([P, SUBS, 2, E]),
                                     ACT.Copy).then_inc(rows_doubled, 1)

            def split_high(s):
                act.wait_ge(k_landed[s % STAGE_SLOTS], 32 * (s // STAGE_SLOTS + 1))
                lo, hi = s * STAGE_COLS, min((s + 1) * STAGE_COLS, KW_COLS)
                nc.scalar.activation(kw[:, lo:hi], k_raw[:, s % STAGE_SLOTS, 0:hi - lo], ACT.Copy).then_inc(k_high, 1)

            def copy_field(c, f, first):
                act.wait_ge(xt_ready, c * FIELDS + f + 1)
                xt, g = xt_ps[f % 2], f % FIELDS // 2
                side = slice(64, 128) if f % 2 else slice(0, 64)
                if first and f == 2 * RAW_UNDER:
                    act.wait_ge(k_ready, STAGES)
                if f >= FIELDS:
                    act.wait_ge(prod_ready, c * NU + UNIT_AT[("full", g, GROUPS - 1)] + 1)
                if f % FIELDS == 0:
                    nc.scalar.activation(x_pair[side, g, :], xt[side, :], ACT.Copy).then_inc(x_copied, 1)
                    return
                if g < GROUPS - 1:
                    nc.scalar.activation(x_pair[side, g, :], xt[side, :], ACT.Copy)
                elif f == FIELDS - 1:
                    act.wait_ge(z_stored, (c * KT + KT - 1) * 16)
                    nc.scalar.activation(z_out[side, :], xt[side, :], ACT.Copy)
                if f >= AHEAD and slot_free_after(f) is not None:
                    act.wait_ge(t_ready, c * NU + slot_free_after(f) + 1)
                nc.scalar.activation(x_high[:, SLOT_OF[f % FIELDS], :], xt[:, :], ACT.Copy).then_inc(x_copied, 1)

            def copy_z(c, k, first):
                last_sum = min((k + 1) * PER_TILE, len(SUMS)) - 1
                act.wait_ge(prod_used, c * NU + SUMS[last_sum][0] + 1)
                if not first or k >= 1:
                    act.wait_ge(z_stored, (c * KT + k) * 16)
                nc.scalar.activation(z_out[:, :], z_ps[k % 2][:, :], ACT.Copy).then_inc(z_copied, 1)

            def chunk(c, first):
                staged, issued, copied = FIRST_STAGES[-1], 0, 0
                assert SUMS[(KT - 1) * PER_TILE - 1][0] + 3 < [e for e in EVENTS[:EVENTS.index(("prep", FIELDS - 1))] if e[0] == "unit"][-1][1]
                for todo, (kind, n) in zip(SUMS_AT, EVENTS):
                    if kind == "unit":
                        while first and staged < stage_target(n):
                            split_high(staged)
                            staged += 1
                    else:
                        copy_field(c, n, first)
                        double_rows(c, n + DOUBLED_AHEAD)
                    if copied < (issued - 1) // PER_TILE:
                        copy_z(c, copied, first)
                        copied += 1
                    issued += len(todo)
                for k in range(copied, KT):
                    copy_z(c, k, first)

            def split_first(f):
                for s in range(FIRST_STAGES[f - 1] if f else 0, FIRST_STAGES[f]):
                    split_high(s)

            split_first(0)
            for f in range(DOUBLED_AHEAD):
                double_rows(0, f)
            for f in range(AHEAD):
                copy_field(0, f, True)
                split_first(f + 1)
                double_rows(0, f + DOUBLED_AHEAD)
            chunk(0, True)
            with act.Fori(1, CHUNKS) as c:
                chunk(c, False)

            def relu_1(n, first):
                for o in range(OT):
                    act.wait_ge(h1_summed, n * OT + o + 1)
                    if not first and o == 0:
                        act.wait_ge(h2_summed, n * HT)
                    nc.scalar.activation(h1_sb[:, o, :], t_ps[o // 2][:, o % 2, :], ACT.Relu,
                                         bias=b1_sb[:, o:o + 1]).then_inc(h1_ready, 1)

            def relu_2(n, first):
                for o in range(HT):
                    act.wait_ge(h2_summed, n * HT + o + 1)
                    if not first and o == 0:
                        act.wait_ge(y_summed, n)
                    nc.scalar.activation(h2_sb[:, o, :], z_ps[o][:, :], ACT.Relu,
                                         bias=b2_sb[:, o:o + 1]).then_inc(h2_ready, 1)

            act.wait_ge(small_landed, 48)
            relu_1(0, True)
            relu_2(0, True)
            with act.Fori(1, CHUNKS - 1) as n:
                relu_1(n, False)
                relu_2(n, False)
            relu_1(CHUNKS - 1, False)
            relu_2(CHUNKS - 1, False)

        @block.vector
        def _(dve):
            def split_low(s):
                lo, hi = s * STAGE_COLS, min((s + 1) * STAGE_COLS, KW_COLS)
                dve.wait_ge(k_high, s + 1)
                nc.vector.tensor_tensor(kw[64:128, lo:hi], k_raw[64:128, s % STAGE_SLOTS, 0:hi - lo],
                                        kw[64:128, lo:hi].bitcast(F32), ALU.subtract).then_inc(k_ready, 1)

            def low_part(c, f):
                dve.wait_ge(x_copied, c * FIELDS + f + 1)
                if f % FIELDS == 0:
                    dve.sem_inc(x_ready, 1)
                    return
                slot = SLOT_OF[f % FIELDS]
                nc.vector.tensor_tensor(x_low[:, slot, :], xt_ps[f % 2][:, :], x_high[:, slot, :].bitcast(F32),
                                        ALU.subtract).then_inc(x_ready, 1)

            def multiply(c, n, first):
                dve.wait_ge(t_ready, c * NU + n + 1)
                if not first or n >= PROD_SLOTS:
                    dve.wait_ge(prod_used, c * NU + n - PROD_SLOTS + 1)
                if UNITS[n][0] == "diag":
                    h = UNITS[n][1]
                    x_odd = x_pair[64:128, 2 * h + 1, :] if 2 * h + 1 < GROUPS - 1 else z_out[64:128, :]
                    nc.vector.tensor_tensor(prod[0:64, n % PROD_SLOTS, 0, :], t_ps[n % 2][0:64, 0, :],
                                            x_pair[0:64, 2 * h, :], ALU.mult)
                    nc.vector.tensor_tensor(prod[64:128, n % PROD_SLOTS, 0, :], t_ps[n % 2][64:128, 0, :],
                                            x_odd, ALU.mult).then_inc(prod_ready, 1)
                else:
                    x_i = x_pair[:, UNITS[n][1]:UNITS[n][1] + 1, :].to_broadcast([P, 2, CHUNK])
                    nc.vector.tensor_tensor(prod[:, n % PROD_SLOTS, :, :], t_ps[n % 2][:, :, :], x_i,
                                            ALU.mult).then_inc(prod_ready, 1)

            def chunk(c, first):
                staged = FIRST_STAGES[-1]
                for kind, n in VECTOR_EVENTS:
                    if kind == "unit":
                        while first and staged < stage_target(n):
                            split_low(staged)
                            staged += 1
                        multiply(c, n, first)
                    else:
                        low_part(c, n)

            nc.vector.memset(sel[:, :], 0.0).then_inc(sel_zeros_set, 1)
            dve.wait_ge(sel_zeros_set, 1)
            nc.vector.memset(sel[0:64, SEL_ROWS - 2:SEL_ROWS - 1], 1.0).then_inc(sel_set, 1)
            nc.vector.memset(sel[64:128, SEL_ROWS - 1:SEL_ROWS], 1.0).then_inc(sel_set, 1)
            for f in range(AHEAD):
                for s in range(FIRST_STAGES[f - 1] if f else 0, FIRST_STAGES[f]):
                    split_low(s)
                low_part(0, f)
            for s in range(FIRST_STAGES[AHEAD - 1], FIRST_STAGES[AHEAD]):
                split_low(s)
            chunk(0, True)
            with dve.Fori(1, CHUNKS) as c:
                chunk(c, False)
            with dve.Fori(0, CHUNKS) as n:
                dve.wait_ge(y_summed, n + 1)
                nc.vector.tensor_copy(y_sb[0:1, bass.ds(n * CHUNK, CHUNK)], xt_ps[0][0:1, :]).then_inc(y_ready, 1)

        @block.tensor
        def _(pe):
            def transpose(c, f, first):
                pe.wait_ge(rows_doubled, c * FIELDS + f + 1)
                if not first or f >= 2:
                    pe.wait_ge(x_ready, c * FIELDS + f - 1)
                for t in range(SUBS):
                    last = nc.tensor.transpose(xt_ps[f % 2][:, t * P:(t + 1) * P],
                                               rows_twice[:, f % TWICE_SLOTS, t, :, :].rearrange("p a e -> p (a e)"),
                                               ident[:, :])
                last.then_inc(xt_ready, 1)

            def contract(c, n, first):
                u = UNITS[n]
                if not first or n >= 2:
                    pe.wait_ge(prod_ready, c * NU + n - 1)
                if n == 0 or GROUP_OF[n] != GROUP_OF[n - 1]:
                    pe.wait_ge(x_ready, c * FIELDS + 2 * GROUP_OF[n] + 2)
                if first:
                    pe.wait_ge(k_ready, stages_of(n))
                for x in range(2):
                    diag = u[0] == "diag"
                    at = COL_OF[n] + (E if diag else P) * x
                    k_part = kw[:, at:at + P]
                    out = t_ps[n % 2][:, 0 if diag else x, :]
                    slot = SLOT_OF[4 * u[1] + 1 + x if diag else 2 * u[2] + x]
                    nc.tensor.matmul(out, k_part, x_high[:, slot, :], start=not (diag and x), stop=False)
                    last = nc.tensor.matmul(out, k_part, x_low[:, slot, :], start=False, stop=not (diag and not x))
                last.then_inc(t_ready, 1)

            def sum_over_e(c, m, first):
                n, x = SUMS[m]
                k, q, r = m // PER_TILE, m % 4, m % PER_TILE // 4
                if m % PER_TILE == 0 and not (first and k < 2):
                    pe.wait_ge(z_copied, c * KT + k - 1)
                if x == 0:
                    pe.wait_ge(prod_ready, c * NU + n + 1)
                mm = nc.tensor.matmul(z_ps[k % 2][SEL_ROWS * q:SEL_ROWS * (q + 1), :],
                                      sel[:, SEL_ROWS - 2 - 2 * r:2 * SEL_ROWS - 2 - 2 * r], prod[:, n % PROD_SLOTS, x, :],
                                      start=r == 0, stop=m + 4 >= len(SUMS) or r == PER_TILE // 4 - 1)
                if m == len(SUMS) - 1 or SUMS[m + 1][0] != n:
                    mm.then_inc(prod_used, 1)

            def chunk(c, first):
                for todo, (kind, n) in zip(SUMS_AT, EVENTS):
                    if kind == "unit":
                        contract(c, n, first)
                    else:
                        transpose(c, n, first)
                    for m in todo:
                        sum_over_e(c, m, first)
                for m in SUMS_LEFT:
                    sum_over_e(c, m, first)

            pe.wait_ge(ident_set, 1)
            pe.wait_ge(sel_set, 2)
            for f in range(AHEAD):
                transpose(0, f, True)
            chunk(0, True)
            with pe.Fori(1, CHUNKS) as c:
                chunk(c, False)

            def layer_1(n, first):
                for o in range(OT):
                    if not first:
                        pe.wait_ge(h1_ready, (n - 1) * OT + o + 1)
                    for k in range(KT):
                        last = nc.tensor.matmul(t_ps[o // 2][:, o % 2, :], w1_sb[:, k, o * P:(o + 1) * P],
                                                z_in[:, n, k, :], start=k == 0, stop=k == KT - 1)
                    last.then_inc(h1_summed, 1)

            def layer_2(n, first):
                pe.wait_ge(h1_ready, (n + 1) * OT)
                for o in range(HT):
                    if not first:
                        pe.wait_ge(h2_ready, (n - 1) * HT + o + 1)
                    for k in range(OT):
                        last = nc.tensor.matmul(z_ps[o][:, :], w2_sb[:, k, o * P:(o + 1) * P], h1_sb[:, k, :],
                                                start=k == 0, stop=k == OT - 1)
                    last.then_inc(h2_summed, 1)

            def layer_3(n, first):
                pe.wait_ge(h2_ready, (n + 1) * HT)
                if not first:
                    pe.wait_ge(y_ready, n)
                for k in range(HT):
                    last = nc.tensor.matmul(xt_ps[0][0:1, :], w3_sb[:, k:k + 1], h2_sb[:, k, :],
                                            start=k == 0, stop=k == HT - 1)
                last.then_inc(y_summed, 1)

            pe.wait_ge(mlp_landed, 16 * MLP_LOADS)
            pe.wait_ge(z_copied, CHUNKS * KT)
            pe.wait_ge(x_ready, CHUNKS * FIELDS + AHEAD)
            pe.wait_ge(small_landed, 48)
            layer_1(0, True)
            layer_1(1, False)
            layer_2(0, True)
            layer_3(0, True)
            with pe.Fori(2, CHUNKS - 1) as n:
                layer_1(n, False)
                layer_2(n - 1, False)
                layer_3(n - 1, False)
            pe.wait_ge(z_last_landed, 16 * Z_LOADS)
            layer_1(CHUNKS - 1, False)
            for n in range(CHUNKS - 2, CHUNKS):
                layer_2(n, False)
                layer_3(n, False)


def kernel(**inputs):
    import numpy as np
    import concourse.bacc as bacc
    from concourse.bass_utils import run_bass_kernel_spmd

    ids = np.asarray(inputs["ids"])
    by_chunk = ids.reshape(CHUNKS, SUBS, P, 2, FIELDS // 2).transpose(0, 3, 2, 4, 1)
    by_chunk = by_chunk.reshape(CHUNKS, 2, P, FIELDS // 2 * SUBS)
    by_chunk = np.concatenate([by_chunk, by_chunk[:1]], axis=0)

    pair_at = {}
    for n, (i, j) in enumerate(zip(*np.triu_indices(FIELDS, k=1))):
        pair_at[int(i), int(j)] = n

    k = np.asarray(inputs["L0_rec_kernel"])
    parts, zeros = [], np.zeros((E, E), k.dtype)
    for n, u in enumerate(UNITS):
        if u[0] == "diag":
            first, second = (k[:, pair_at[pair]] for pair in pairs_of(n, 0))
            parts += [first, zeros, second.T]
        else:
            parts += [k[:, pair_at[pair]] for x in range(2) for pair in pairs_of(n, x)]

    w1 = np.asarray(inputs["W_top1"])
    order = np.zeros((KT, 4, SEL_ROWS), np.int64)
    for m, (n, x) in enumerate(SUMS):
        for y, pair in enumerate(pairs_of(n, x)):
            order[m // PER_TILE, m % 4, 2 * (m % PER_TILE // 4) + y] = pair_at[pair]
    order[KT - 1, :, LAST_ROWS:] = PAIRS + np.arange(DENSE).reshape(4, DENSE // 4)

    def tiles(a, n):
        return np.ascontiguousarray(a.reshape(n, P, -1).transpose(1, 0, 2))

    arrays = {
        "ids": by_chunk,
        "dense_t": np.asarray(inputs["dense_ctx"]).T,
        "k_units": np.concatenate(parts, axis=1),
        "w1": tiles(w1[order.reshape(-1)], KT),
        "b1": np.asarray(inputs["b_top1"]).reshape(OT, P).T,
        "w2": tiles(np.asarray(inputs["W_top2"]), OT),
        "b2": np.asarray(inputs["b_top2"]).reshape(HT, P).T,
        "w3": np.asarray(inputs["W_top3"]).reshape(HT, P).T,
    }
    arrays |= {f"tbl_{f}": np.asarray(inputs[f"tbl_{f}"]) for f in range(FIELDS)}
    arrays = {name: np.ascontiguousarray(a) for name, a in arrays.items()}

    nc = bacc.Bacc("TRN2", target_bir_lowering=False, num_devices=1)
    ap = {name: nc.dram_tensor(f"{name}_dram", a.shape, mybir.dt.from_np(a.dtype), kind="ExternalInput").ap()
          for name, a in arrays.items()}
    y = nc.dram_tensor("y_dram", (1, BATCH), F32, kind="ExternalOutput").ap()
    tower_kernel(nc, ap["ids"], ap["dense_t"], ap["k_units"], ap["w1"], ap["b1"], ap["w2"], ap["b2"], ap["w3"],
                 [ap[f"tbl_{f}"] for f in range(FIELDS)], y)
    r = run_bass_kernel_spmd(nc, [{f"{name}_dram": a for name, a in arrays.items()}], core_ids=[0])
    return r.results[0]["y_dram"].reshape(BATCH, 1)
```

```python
from contextlib import ExitStack

import concourse.bass as bass
from concourse import mybir

F32 = mybir.dt.float32
F32R = mybir.dt.float32r
I32 = mybir.dt.int32
ALU = mybir.AluOpType
ACT = mybir.ActivationFunctionType

P = 128
BATCH, FIELDS, E = 2048, 32, 64
PAIRS = FIELDS * (FIELDS - 1) // 2
DENSE, H1, H2 = 16, 512, 256
CHUNK = 512
CHUNKS = BATCH // CHUNK
SUBS = CHUNK // P
GROUPS = FIELDS // 2

ROW_SLOTS = 8
TWICE_SLOTS = 2
SPLIT_SLOTS = 5
PROD_SLOTS = 4
RAW_UNDER = 9
STAGE_SLOTS = GROUPS - 1 - RAW_UNDER
AHEAD = 6
FIRST_AHEAD = 5
DOUBLED_AHEAD = 2
EARLY_AT = {6: 0, 7: 1, 8: 3, 9: 4, 10: 6, 11: 8}
GATHERED_AT = {5: 1, 6: 1, 7: 3, 8: 3, 9: 6, 10: 7, 11: 10, 12: 11, 13: 14, 14: 17, 15: 20}
NEXT_AT = [3, 5, 8, 10, 12, 14]
WARM = {0: 24, 1: 7, 2: 12, 3: 12, 4: 12, 6: 9, 7: 3, 8: 9, 10: 3}
DELAY = 1
FIRST_STAGES = [6, 11, 15, 19, 24, 28]
FIELD_STAGES = {5: 4, 6: 3, 7: 4, 8: 3, 9: 3, 10: 3, 11: 3}
UNIT_STAGES = 0.5

KT = H1 // P
OT = H1 // P
HT = H2 // P
SEL_ROWS = 32
LAST_ROWS = SEL_ROWS - DENSE // 4


def plan_units():
    units = []
    for g in range(1, GROUPS):
        if g % 2:
            units.append(("diag", g // 2))
        units += [("full", a, g) for a in range(g)]
    return units


UNITS = plan_units()
NU = len(UNITS)
UNIT_COLS = [3 * E if u[0] == "diag" else 4 * E for u in UNITS]
COL_OF = [sum(UNIT_COLS[:n]) for n in range(NU)]
KW_COLS = sum(UNIT_COLS)
STAGE_COLS = 8 * E
STAGES = -(-KW_COLS // STAGE_COLS)
UNIT_AT = {u: n for n, u in enumerate(UNITS)}
GROUP_OF = [2 * u[1] + 1 if u[0] == "diag" else u[2] for u in UNITS]


def sum_plan():
    return [(n, x) for n, u in enumerate(UNITS) for x in range(1 if u[0] == "diag" else 2)]


SUMS = sum_plan()
PER_TILE = 4 * SEL_ROWS // 2


def pairs_of(n, x):
    u = UNITS[n]
    if u[0] == "diag":
        return [(4 * u[1], 4 * u[1] + 1), (4 * u[1] + 2, 4 * u[1] + 3)]
    return [(2 * u[1], 2 * u[2] + x), (2 * u[1] + 1, 2 * u[2] + x)]


def plan_slots():
    group_slots = {1: (2, 4), 2: (0, 3), 3: (1, 2), 4: (4, 0), 5: (3, 1), 6: (2, 4)}
    slots = [None, 1]
    for g in range(1, GROUPS):
        slots += group_slots.get(g, (0, 3) if g % 2 else (1, 2))
    return slots


SLOT_OF = plan_slots()


def last_unit_of(f):
    return UNIT_AT[("diag", f // 4)] if f % 4 == 1 else UNIT_AT[("full", f // 2 - 1, f // 2)]


def slot_free_after(f):
    for before in range(f - 1, max(0, f - FIELDS), -1):
        if SLOT_OF[before % FIELDS] == SLOT_OF[f % FIELDS]:
            return last_unit_of(before) if before < FIELDS else None
    return None


def plan_events(early, start, end):
    after = {}
    for f in range(start, end):
        before = f // 2 - 1
        if f in early:
            at = early[f]
        elif f >= FIELDS:
            at = UNIT_AT[("full", 0, GROUPS - 1)] + NEXT_AT[f - FIELDS]
        elif before > 6:
            at = UNIT_AT[("full", 0, before)] + (before // 2 + 1 if f % 2 else 2)
        else:
            at = GROUP_OF.index(before) + (2 if f % 2 else 0)
        if f not in early and f < FIELDS:
            at += at % 2
        after.setdefault(at, []).append(f)
    events = []
    for n in range(NU):
        events += [("unit", n)] + [("prep", f) for f in after.get(n, [])]
    return events


def plan_vector_events(events):
    at, unit = {}, 0
    for kind, n in events:
        if kind == "unit":
            unit = n
        else:
            at[n] = unit
    order = [e for e in events if e[0] == "unit"]
    for f in reversed(at):
        group_starts = GROUP_OF.index(f // 2) if f < FIELDS else NU
        late = max(at[f], min(at[f] + DELAY, group_starts - 2, at.get(f + 2, NU)))
        order.insert(order.index(("unit", late)) + 1, ("prep", f))
    return order


def plan_sums(events):
    at, issued = [], 0
    for kind, n in events:
        ready = sum(s[0] <= n - 2 for s in SUMS) if kind == "unit" else 0
        todo = []
        while ready - issued >= 4:
            todo += range(issued, issued + 4)
            issued += 4
        if kind == "unit" and issued < sum(s[0] <= n - PROD_SLOTS + 1 for s in SUMS):
            todo += range(issued, ready)
            issued = ready
        at.append(todo)
    return at, list(range(issued, len(SUMS)))


class Plan:
    def __init__(self, early, start, end):
        self.events = plan_events(early, start, end)
        self.vector_events = plan_vector_events(self.events)
        self.sums_at, self.sums_left = plan_sums(self.events)


FIRST = Plan(GATHERED_AT, FIRST_AHEAD, FIELDS + AHEAD)
MIDDLE = Plan(EARLY_AT, AHEAD, FIELDS + AHEAD)
LAST = Plan(EARLY_AT, AHEAD, FIELDS)


def stages_of(n):
    return -(-(COL_OF[n] + UNIT_COLS[n]) // STAGE_COLS)


def plan_stages():
    done, count = {}, FIRST_STAGES[-1]
    for kind, n in FIRST.events[:FIRST.events.index(("prep", 2 * RAW_UNDER))]:
        if kind == "prep":
            count += FIELD_STAGES.get(n, 0)
        elif n > GATHERED_AT[max(FIELD_STAGES)]:
            count += UNIT_STAGES
        done[kind, n] = min(STAGES, int(count))
    done[kind, n] = STAGES
    return done


STAGES_DONE = plan_stages()
Z_LOADS = 5
MLP_LOADS = 2 + 4 + (CHUNKS - 1) * Z_LOADS


def tower_kernel(nc, ids, dense_t, k_units, w1, b1, w2, b2, w3, tables, y_out):
    ctx = ExitStack()
    with ctx:
        def sb(name, shape, dt=F32):
            return ctx.enter_context(nc.sbuf_tensor(name, shape, dt))

        def ps(name, shape):
            return ctx.enter_context(nc.psum_tensor(name, shape, F32))

        def sem(name):
            return ctx.enter_context(nc.semaphore(name))

        kw_at = -(-nc.sbuf_base // 32) * 32
        kw = sb("kw", [P, KW_COLS], F32R)
        x_pair_at = -(-nc.sbuf_base // 32) * 32
        x_pair = sb("x_pair", [P, GROUPS - 1, CHUNK])
        z_out = sb("z_out", [P, CHUNK])
        x_high = sb("x_high", [P, SPLIT_SLOTS, CHUNK], F32R)
        x_low = sb("x_low", [P, SPLIT_SLOTS, CHUNK], F32R)
        prod = sb("prod", [P, PROD_SLOTS, 2, CHUNK])
        rows = sb("rows", [P, ROW_SLOTS, SUBS, E])
        rows_twice = sb("rows_twice", [P, TWICE_SLOTS, SUBS, 2, E])
        idx = sb("idx", [P, 2, FIELDS // 2 * SUBS], I32)
        ident = sb("ident", [P, P])
        sel = sb("sel", [P, 2 * SEL_ROWS])
        b1_sb = sb("b1_sb", [P, OT])
        b2_sb = sb("b2_sb", [P, HT])
        w3_sb = sb("w3_sb", [P, HT])

        k_raw = nc.alloc_sbuf_tensor_at("k_raw", [P, STAGE_SLOTS, STAGE_COLS], F32,
                                        offset=x_pair_at + RAW_UNDER * CHUNK * 4)

        taken = [kw_at]

        def over_kw(name, shape):
            t = nc.alloc_sbuf_tensor_at(name, shape, F32, offset=taken[0])
            n = 4
            for d in shape[1:]:
                n *= d
            taken[0] += n
            return t

        z_in = over_kw("z_in", [P, CHUNKS, KT, CHUNK])
        w1_sb = over_kw("w1_sb", [P, KT, H1])
        w2_sb = over_kw("w2_sb", [P, OT, H2])
        units_under_loads = sum(4 * col < taken[0] - kw_at for col in COL_OF)
        h1_sb = over_kw("h1_sb", [P, CHUNKS, OT, CHUNK])
        h2_sb = over_kw("h2_sb", [P, CHUNKS, HT, CHUNK])
        y_sb = over_kw("y_sb", [P, CHUNK])
        assert taken[0] - kw_at <= KW_COLS * 4

        z_dram = nc.dram_tensor("z_scratch", [CHUNKS, KT, P, CHUNK], F32, kind="Internal").ap()

        t_ps = [ps(f"t_ps{i}", [P, 2, CHUNK]) for i in range(2)]
        z_ps = [ps(f"z_ps{i}", [P, CHUNK]) for i in range(2)]
        xt_ps = [ps(f"xt_ps{i}", [P, CHUNK]) for i in range(2)]

        idx_landed = [sem(f"idx_landed{i}") for i in range(2)]
        rows_landed = [sem(f"rows_landed{i}") for i in range(ROW_SLOTS)]
        k_landed = [sem(f"k_landed{i}") for i in range(STAGE_SLOTS)]
        small_landed = sem("small_landed")
        zeros_set = sem("zeros_set")
        ident_set = sem("ident_set")
        sel_zeros_set = sem("sel_zeros_set")
        sel_set = sem("sel_set")
        field_turn = sem("field_turn")
        rows_doubled = sem("rows_doubled")
        xt_ready = sem("xt_ready")
        x_copied = sem("x_copied")
        x_ready = sem("x_ready")
        k_high = sem("k_high")
        k_ready = sem("k_ready")
        t_ready = sem("t_ready")
        prod_ready = sem("prod_ready")
        prod_used = sem("prod_used")
        z_copied = sem("z_copied")
        z_stored = sem("z_stored")
        mlp_landed = sem("mlp_landed")
        z_last_landed = sem("z_last_landed")
        h1_summed = sem("h1_summed")
        h1_ready = sem("h1_ready")
        h2_summed = sem("h2_summed")
        h2_ready = sem("h2_ready")
        y_summed = sem("y_summed")
        y_ready = sem("y_ready")
        y_stored = sem("y_stored")

        block = ctx.enter_context(nc.Block())

        @block.sync
        def _(sp):
            def load_idx(c, half):
                sp.dma_start(idx[:, half, :], ids[c, half]).then_inc(idx_landed[half], 16)

            for half in range(2):
                load_idx(0, half)
            for s in range(STAGES):
                slot = s % STAGE_SLOTS
                if s >= STAGE_SLOTS:
                    sp.wait_ge(k_ready, s - STAGE_SLOTS + 1)
                lo, hi = s * STAGE_COLS, min((s + 1) * STAGE_COLS, KW_COLS)
                sp.dma_start(k_raw[:, slot, 0:hi - lo], k_units[:, lo:hi]).then_inc(k_landed[slot], 16)
                if s == 4:
                    sp.dma_start(b1_sb[:, :], b1).then_inc(small_landed, 16)
                    sp.dma_start(b2_sb[:, :], b2).then_inc(small_landed, 16)
                    sp.dma_start(w3_sb[:, :], w3).then_inc(small_landed, 16)

            def store_z(c, k):
                sp.wait_ge(z_copied, c * KT + k + 1)
                sp.dma_start(z_dram[c, k], z_out[:, :]).then_inc(z_stored, 16)

            def next_idx(c, half):
                sp.wait_ge(rows_doubled, c * FIELDS + (half + 1) * (FIELDS // 2))
                load_idx(c + 1, half)

            def load_z(c, landed):
                sp.dma_start(z_in[:, c, 0:KT - 1, :], z_dram[c, 0:KT - 1].rearrange("k p b -> p k b")
                             ).then_inc(landed, 16)
                for q in range(4):
                    own = slice(SEL_ROWS * q, SEL_ROWS * q + LAST_ROWS)
                    sp.dma_start(z_in[own, c, KT - 1, :], z_dram[c, KT - 1, own, :]).then_inc(landed, 16)

            with sp.Fori(0, CHUNKS - 1) as c:
                store_z(c, 0)
                next_idx(c, 0)
                store_z(c, 1)
                store_z(c, 2)
                next_idx(c, 1)
                store_z(c, 3)
            store_z(CHUNKS - 1, 0)
            store_z(CHUNKS - 1, 1)
            sp.wait_ge(t_ready, (CHUNKS - 1) * NU + units_under_loads)
            sp.wait_ge(z_stored, (CHUNKS - 1) * KT * 16)
            sp.dma_start(w1_sb[:, :, :], w1).then_inc(mlp_landed, 16)
            sp.dma_start(w2_sb[:, :, :], w2).then_inc(mlp_landed, 16)
            for q in range(4):
                sp.dma_start(z_in[SEL_ROWS * q + LAST_ROWS:SEL_ROWS * (q + 1), :, KT - 1, :],
                             dense_t[q * (DENSE // 4):(q + 1) * (DENSE // 4), :].rearrange("d (c b) -> d c b", c=CHUNKS)
                             ).then_inc(mlp_landed, 16)
            for c in range(CHUNKS - 1):
                load_z(c, mlp_landed)
            store_z(CHUNKS - 1, 2)
            store_z(CHUNKS - 1, 3)
            sp.wait_ge(z_stored, CHUNKS * KT * 16)
            load_z(CHUNKS - 1, z_last_landed)

            sp.wait_ge(y_ready, 1)
            sp.dma_start(y_out, y_sb[0:P:SEL_ROWS, :]).then_inc(y_stored, 16)
            sp.wait_ge(y_stored, 16)

        @block.gpsimd
        def _(pool):
            nc.gpsimd.memset(ident[:, :], 0.0).then_inc(zeros_set, 1)
            pool.wait_ge(zeros_set, 1)
            nc.gpsimd.affine_select(out=ident[:, :], in_=ident[:, :], compare_op=ALU.not_equal, fill=1.0,
                                    base=0, pattern=[[-1, P]], channel_multiplier=1).then_inc(ident_set, 1)

            def gather(c, f, first):
                half, at = f // (FIELDS // 2), f % (FIELDS // 2)
                if at == 0:
                    pool.wait_ge(idx_landed[half], c * 16 + 16)
                if not first or f >= ROW_SLOTS:
                    pool.wait_ge(rows_doubled, c * FIELDS + f - ROW_SLOTS + 1)
                pool.sem_inc(field_turn, 1)
                for t in range(SUBS):
                    nc.gpsimd.indirect_dma_start(
                        out=rows[:, f % ROW_SLOTS, t, :], out_offset=None, in_=tables[f],
                        in_offset=bass.IndirectOffsetOnAxis(ap=idx[:, half, at * SUBS + t:at * SUBS + t + 1], axis=0),
                    ).then_inc(rows_landed[f % ROW_SLOTS], 16)

            for f in range(FIELDS):
                gather(0, f, True)
            with pool.Fori(1, CHUNKS) as c:
                for f in range(FIELDS):
                    gather(c, f, False)

        @block.scalar
        def _(act):
            def double_rows(c, f):
                gathers = (c * (FIELDS // ROW_SLOTS) + f // ROW_SLOTS + 1) * SUBS
                act.wait_ge(rows_landed[f % ROW_SLOTS], gathers * 16)
                nc.scalar.activation(rows_twice[:, f % TWICE_SLOTS, :, :, :],
                                     rows[:, f % ROW_SLOTS, :, None, :].to_broadcast([P, SUBS, 2, E]),
                                     ACT.Copy).then_inc(rows_doubled, 1)

            def split_high(s):
                act.wait_ge(k_landed[s % STAGE_SLOTS], 16 * (s // STAGE_SLOTS + 1))
                lo, hi = s * STAGE_COLS, min((s + 1) * STAGE_COLS, KW_COLS)
                nc.scalar.activation(kw[:, lo:hi], k_raw[:, s % STAGE_SLOTS, 0:hi - lo], ACT.Copy).then_inc(k_high, 1)

            def copy_field(c, f, first):
                act.wait_ge(xt_ready, c * FIELDS + f + 1)
                xt, g = xt_ps[f % 2], f % FIELDS // 2
                side = slice(64, 128) if f % 2 else slice(0, 64)
                if first and f == 2 * RAW_UNDER:
                    act.wait_ge(k_ready, STAGES)
                if f >= FIELDS:
                    act.wait_ge(prod_ready, c * NU + UNIT_AT[("full", g, GROUPS - 1)] + 1)
                if f % FIELDS == 0:
                    nc.scalar.activation(x_pair[side, g, :], xt[side, :], ACT.Copy).then_inc(x_copied, 1)
                    return
                if g < GROUPS - 1:
                    nc.scalar.activation(x_pair[side, g, :], xt[side, :], ACT.Copy)
                elif f == FIELDS - 1:
                    act.wait_ge(z_stored, (c * KT + KT - 1) * 16)
                    nc.scalar.activation(z_out[side, :], xt[side, :], ACT.Copy)
                if f >= AHEAD and slot_free_after(f) is not None:
                    act.wait_ge(t_ready, c * NU + slot_free_after(f) + 1)
                nc.scalar.activation(x_high[:, SLOT_OF[f % FIELDS], :], xt[:, :], ACT.Copy).then_inc(x_copied, 1)

            def copy_z(c, k, first):
                last_sum = min((k + 1) * PER_TILE, len(SUMS)) - 1
                act.wait_ge(prod_used, c * NU + SUMS[last_sum][0] + 1)
                if not first or k >= 1:
                    act.wait_ge(z_stored, (c * KT + k) * 16)
                nc.scalar.activation(z_out[:, :], z_ps[k % 2][:, :], ACT.Copy).then_inc(z_copied, 1)

            def chunk(c, plan):
                first = plan is FIRST
                staged, issued, copied = FIRST_STAGES[-1], 0, 0
                for todo, (kind, n) in zip(plan.sums_at, plan.events):
                    if kind == "prep":
                        copy_field(c, n, first)
                        if plan is not LAST or n + DOUBLED_AHEAD < FIELDS:
                            double_rows(c, n + DOUBLED_AHEAD)
                    while first and staged < STAGES_DONE.get((kind, n), 0):
                        split_high(staged)
                        staged += 1
                    if copied < (issued - 1) // PER_TILE:
                        copy_z(c, copied, first)
                        copied += 1
                    issued += len(todo)
                for k in range(copied, KT):
                    copy_z(c, k, first)

            def split_first(f):
                for s in range(FIRST_STAGES[f - 1] if f else 0, FIRST_STAGES[f]):
                    split_high(s)

            split_first(0)
            for f in range(DOUBLED_AHEAD):
                double_rows(0, f)
            for f in range(FIRST_AHEAD):
                copy_field(0, f, True)
                split_first(f + 1)
                double_rows(0, f + DOUBLED_AHEAD)
            chunk(0, FIRST)
            with act.Fori(1, CHUNKS - 1) as c:
                chunk(c, MIDDLE)
            chunk(CHUNKS - 1, LAST)

            def relu_1(n):
                for o in range(OT):
                    act.wait_ge(h1_summed, n * OT + o + 1)
                    nc.scalar.activation(h1_sb[:, n, o, :], t_ps[o // 2][:, o % 2, :], ACT.Relu,
                                         bias=b1_sb[:, o:o + 1]).then_inc(h1_ready, 1)

            def relu_2(n):
                for o in range(HT):
                    act.wait_ge(h2_summed, n * HT + o + 1)
                    nc.scalar.activation(h2_sb[:, n, o, :], z_ps[o][:, :], ACT.Relu,
                                         bias=b2_sb[:, o:o + 1]).then_inc(h2_ready, 1)

            act.wait_ge(small_landed, 48)
            relu_1(0)
            with act.Fori(1, CHUNKS) as n:
                relu_1(n)
                relu_2(n - 1)
            relu_2(CHUNKS - 1)

        @block.vector
        def _(dve):
            def split_low(s):
                lo, hi = s * STAGE_COLS, min((s + 1) * STAGE_COLS, KW_COLS)
                dve.wait_ge(k_high, s + 1)
                nc.vector.tensor_tensor(kw[64:128, lo:hi], k_raw[64:128, s % STAGE_SLOTS, 0:hi - lo],
                                        kw[64:128, lo:hi].bitcast(F32), ALU.subtract).then_inc(k_ready, 1)

            def low_part(c, f):
                dve.wait_ge(x_copied, c * FIELDS + f + 1)
                if f % FIELDS == 0:
                    dve.sem_inc(x_ready, 1)
                    return
                slot = SLOT_OF[f % FIELDS]
                nc.vector.tensor_tensor(x_low[:, slot, :], xt_ps[f % 2][:, :], x_high[:, slot, :].bitcast(F32),
                                        ALU.subtract).then_inc(x_ready, 1)

            def multiply(c, n, first):
                dve.wait_ge(t_ready, c * NU + n + 1)
                if not first or n >= PROD_SLOTS:
                    dve.wait_ge(prod_used, c * NU + n - PROD_SLOTS + 1)
                if UNITS[n][0] == "diag":
                    h = UNITS[n][1]
                    x_odd = x_pair[64:128, 2 * h + 1, :] if 2 * h + 1 < GROUPS - 1 else z_out[64:128, :]
                    nc.vector.tensor_tensor(prod[0:64, n % PROD_SLOTS, 0, :], t_ps[n % 2][0:64, 0, :],
                                            x_pair[0:64, 2 * h, :], ALU.mult)
                    nc.vector.tensor_tensor(prod[64:128, n % PROD_SLOTS, 0, :], t_ps[n % 2][64:128, 0, :],
                                            x_odd, ALU.mult).then_inc(prod_ready, 1)
                else:
                    x_i = x_pair[:, UNITS[n][1]:UNITS[n][1] + 1, :].to_broadcast([P, 2, CHUNK])
                    nc.vector.tensor_tensor(prod[:, n % PROD_SLOTS, :, :], t_ps[n % 2][:, :, :], x_i,
                                            ALU.mult).then_inc(prod_ready, 1)

            def chunk(c, plan):
                first = plan is FIRST
                staged = FIRST_STAGES[-1]
                for kind, n in plan.vector_events:
                    if kind == "unit":
                        multiply(c, n, first)
                    else:
                        low_part(c, n)
                    while first and staged < STAGES_DONE.get((kind, n), 0):
                        split_low(staged)
                        staged += 1

            nc.vector.memset(sel[:, :], 0.0).then_inc(sel_zeros_set, 1)
            dve.wait_ge(sel_zeros_set, 1)
            nc.vector.memset(sel[0:64, SEL_ROWS - 2:SEL_ROWS - 1], 1.0).then_inc(sel_set, 1)
            nc.vector.memset(sel[64:128, SEL_ROWS - 1:SEL_ROWS], 1.0).then_inc(sel_set, 1)
            for f in range(FIRST_AHEAD):
                for s in range(FIRST_STAGES[f - 1] if f else 0, FIRST_STAGES[f]):
                    split_low(s)
                low_part(0, f)
            for s in range(FIRST_STAGES[FIRST_AHEAD - 1], FIRST_STAGES[FIRST_AHEAD]):
                split_low(s)
            chunk(0, FIRST)
            with dve.Fori(1, CHUNKS - 1) as c:
                chunk(c, MIDDLE)
            chunk(CHUNKS - 1, LAST)
            dve.wait_ge(y_summed, 1)
            nc.vector.tensor_copy(y_sb[:, :], xt_ps[0][:, :]).then_inc(y_ready, 1)

        @block.tensor
        def _(pe):
            def transpose(c, f, first):
                pe.wait_ge(rows_doubled, c * FIELDS + f + 1)
                if not first or f >= 2:
                    pe.wait_ge(x_ready, c * FIELDS + f - 1)
                for t in range(SUBS):
                    last = nc.tensor.transpose(xt_ps[f % 2][:, t * P:(t + 1) * P],
                                               rows_twice[:, f % TWICE_SLOTS, t, :, :].rearrange("p a e -> p (a e)"),
                                               ident[:, :])
                last.then_inc(xt_ready, 1)

            def keep_warm(products):
                for _ in range(products):
                    nc.tensor.matmul(z_ps[1][:, 0:P], ident[:, :], ident[:, :], start=True, stop=True)

            def contract(c, n, first):
                u = UNITS[n]
                if not first or n >= 2:
                    pe.wait_ge(prod_ready, c * NU + n - 1)
                if n == 0 or GROUP_OF[n] != GROUP_OF[n - 1]:
                    pe.wait_ge(x_ready, c * FIELDS + 2 * GROUP_OF[n] + 2)
                if first:
                    pe.wait_ge(k_ready, stages_of(n))
                for x in range(2):
                    diag = u[0] == "diag"
                    at = COL_OF[n] + (E if diag else P) * x
                    k_part = kw[:, at:at + P]
                    out = t_ps[n % 2][:, 0 if diag else x, :]
                    slot = SLOT_OF[4 * u[1] + 1 + x if diag else 2 * u[2] + x]
                    nc.tensor.matmul(out, k_part, x_high[:, slot, :], start=not (diag and x), stop=False)
                    last = nc.tensor.matmul(out, k_part, x_low[:, slot, :], start=False, stop=not (diag and not x))
                last.then_inc(t_ready, 1)

            def sum_over_e(c, m, first):
                n, x = SUMS[m]
                k, q, r = m // PER_TILE, m % 4, m % PER_TILE // 4
                if m % PER_TILE == 0 and not (first and k < 2):
                    pe.wait_ge(z_copied, c * KT + k - 1)
                if x == 0:
                    pe.wait_ge(prod_ready, c * NU + n + 1)
                mm = nc.tensor.matmul(z_ps[k % 2][SEL_ROWS * q:SEL_ROWS * (q + 1), :],
                                      sel[:, SEL_ROWS - 2 - 2 * r:2 * SEL_ROWS - 2 - 2 * r],
                                      prod[:, n % PROD_SLOTS, x, :],
                                      start=r == 0, stop=m + 4 >= len(SUMS) or r == PER_TILE // 4 - 1)
                if m == len(SUMS) - 1 or SUMS[m + 1][0] != n:
                    mm.then_inc(prod_used, 1)

            def chunk(c, plan):
                first = plan is FIRST
                for todo, (kind, n) in zip(plan.sums_at, plan.events):
                    if kind == "unit":
                        contract(c, n, first)
                    else:
                        if first:
                            keep_warm(WARM.get(n, 0))
                        transpose(c, n, first)
                    for m in todo:
                        sum_over_e(c, m, first)
                for m in plan.sums_left:
                    sum_over_e(c, m, first)

            pe.wait_ge(ident_set, 1)
            pe.wait_ge(sel_set, 2)
            for f in range(FIRST_AHEAD):
                keep_warm(WARM.get(f, 0))
                transpose(0, f, True)
            chunk(0, FIRST)
            with pe.Fori(1, CHUNKS - 1) as c:
                chunk(c, MIDDLE)
            chunk(CHUNKS - 1, LAST)

            def layer_1(n, first):
                for o in range(OT):
                    if not first:
                        pe.wait_ge(h1_ready, (n - 1) * OT + o + 1)
                    for k in range(KT):
                        last = nc.tensor.matmul(t_ps[o // 2][:, o % 2, :], w1_sb[:, k, o * P:(o + 1) * P],
                                                z_in[:, n, k, :], start=k == 0, stop=k == KT - 1)
                    last.then_inc(h1_summed, 1)

            def layer_2(n, first):
                pe.wait_ge(h1_ready, (n + 1) * OT)
                for o in range(HT):
                    if not first:
                        pe.wait_ge(h2_ready, (n - 1) * HT + o + 1)
                    for k in range(OT):
                        last = nc.tensor.matmul(z_ps[o][:, :], w2_sb[:, k, o * P:(o + 1) * P], h1_sb[:, n, k, :],
                                                start=k == 0, stop=k == OT - 1)
                    last.then_inc(h2_summed, 1)

            def layer_3():
                pe.wait_ge(h2_ready, CHUNKS * HT)
                for k in range(HT):
                    for n in range(CHUNKS):
                        last = nc.tensor.matmul(xt_ps[0][SEL_ROWS * n:SEL_ROWS * (n + 1), :],
                                                w3_sb[:, k:k + 1].to_broadcast([P, SEL_ROWS]), h2_sb[:, n, k, :],
                                                start=k == 0, stop=k == HT - 1)
                last.then_inc(y_summed, 1)

            pe.wait_ge(mlp_landed, 16 * MLP_LOADS)
            pe.wait_ge(z_copied, CHUNKS * KT - 1)
            layer_1(0, True)
            layer_1(1, False)
            pe.wait_ge(z_copied, CHUNKS * KT)
            layer_2(0, True)
            with pe.Fori(2, CHUNKS - 1) as n:
                layer_1(n, False)
                layer_2(n - 1, False)
            pe.wait_ge(z_last_landed, 16 * Z_LOADS)
            layer_1(CHUNKS - 1, False)
            for n in range(CHUNKS - 2, CHUNKS):
                layer_2(n, False)
            pe.wait_ge(small_landed, 48)
            layer_3()


def kernel(**inputs):
    import numpy as np
    import concourse.bacc as bacc
    from concourse.bass_utils import run_bass_kernel_spmd

    ids = np.asarray(inputs["ids"])
    by_chunk = ids.reshape(CHUNKS, SUBS, P, 2, FIELDS // 2).transpose(0, 3, 2, 4, 1)
    by_chunk = by_chunk.reshape(CHUNKS, 2, P, FIELDS // 2 * SUBS)

    pair_at = {}
    for n, (i, j) in enumerate(zip(*np.triu_indices(FIELDS, k=1))):
        pair_at[int(i), int(j)] = n

    k = np.asarray(inputs["L0_rec_kernel"])
    parts, zeros = [], np.zeros((E, E), k.dtype)
    for n, u in enumerate(UNITS):
        if u[0] == "diag":
            first, second = (k[:, pair_at[pair]] for pair in pairs_of(n, 0))
            parts += [first, zeros, second.T]
        else:
            parts += [k[:, pair_at[pair]] for x in range(2) for pair in pairs_of(n, x)]

    w1 = np.asarray(inputs["W_top1"])
    order = np.zeros((KT, 4, SEL_ROWS), np.int64)
    for m, (n, x) in enumerate(SUMS):
        for y, pair in enumerate(pairs_of(n, x)):
            order[m // PER_TILE, m % 4, 2 * (m % PER_TILE // 4) + y] = pair_at[pair]
    order[KT - 1, :, LAST_ROWS:] = PAIRS + np.arange(DENSE).reshape(4, DENSE // 4)

    def tiles(a, n):
        return np.ascontiguousarray(a.reshape(n, P, -1).transpose(1, 0, 2))

    arrays = {
        "ids": by_chunk,
        "dense_t": np.asarray(inputs["dense_ctx"]).T,
        "k_units": np.tile(np.concatenate(parts, axis=1), (2, 1)),
        "w1": tiles(w1[order.reshape(-1)], KT),
        "b1": np.asarray(inputs["b_top1"]).reshape(OT, P).T,
        "w2": tiles(np.asarray(inputs["W_top2"]), OT),
        "b2": np.asarray(inputs["b_top2"]).reshape(HT, P).T,
        "w3": np.asarray(inputs["W_top3"]).reshape(HT, P).T,
    }
    arrays |= {f"tbl_{f}": np.asarray(inputs[f"tbl_{f}"]) for f in range(FIELDS)}
    arrays = {name: np.ascontiguousarray(a) for name, a in arrays.items()}

    nc = bacc.Bacc("TRN2", target_bir_lowering=False, num_devices=1)
    ap = {name: nc.dram_tensor(f"{name}_dram", a.shape, mybir.dt.from_np(a.dtype), kind="ExternalInput").ap()
          for name, a in arrays.items()}
    y = nc.dram_tensor("y_dram", (CHUNKS, CHUNK), F32, kind="ExternalOutput").ap()
    tower_kernel(nc, ap["ids"], ap["dense_t"], ap["k_units"], ap["w1"], ap["b1"], ap["w2"], ap["b2"], ap["w3"],
                 [ap[f"tbl_{f}"] for f in range(FIELDS)], y)
    r = run_bass_kernel_spmd(nc, [{f"{name}_dram": a for name, a in arrays.items()}], core_ids=[0])
    return r.results[0]["y_dram"].reshape(BATCH, 1)
```
